# Optimizing a Trainium2 kernel written in Bass

```python
import numpy as np
import jax
import jax.numpy as jnp

def _softmax(x, axis=-1):
    return jax.nn.softmax(x, axis=axis)

def _gelu(x):
    return jax.nn.gelu(x, approximate=True)

def _silu(x):
    return jax.nn.silu(x)

def _sigmoid(x):
    return jax.nn.sigmoid(x)

def _layernorm(x, axis=-1, eps=1e-05):
    m = jnp.mean(x, axis=axis, keepdims=True)
    v = jnp.var(x, axis=axis, keepdims=True)
    return (x - m) / jnp.sqrt(v + eps)

def _scatter_add(tgt, idx, src, axis=0):
    return tgt.at[idx].add(src)

def _segment_sum(src, seg, n):
    return jax.ops.segment_sum(src, seg, n)
kernel_name = 'mk_decoder_preln_d1_seqx_r8_440bf5'

def setup_inputs(seed: int=0):
    np.random.seed(seed)
    _w = jnp.asarray

    def _rec_inputs():
        import jax
        import jax.numpy as jnp
        _rk = jax.random.key(seed)
        x = -0.0003929 + 0.9999 * jax.random.normal(jax.random.fold_in(_rk, 1), (32, 64, 512), jnp.float32)
        _lenS = 64 - jax.random.randint(jax.random.fold_in(_rk, 7), (32,), 0, max(1, 64 // 4) + 1, jnp.int32)
        _lenS2 = 64 - jax.random.randint(jax.random.fold_in(_rk, 8), (32,), 0, max(1, 64 // 4) + 1, jnp.int32)
        _ctx_1024P = jax.random.normal(jax.random.fold_in(_rk, 11), (32, 16, 128), jnp.float32)
        _ctx_1024c = jax.random.dirichlet(jax.random.fold_in(_rk, 511), 0.3 * jnp.ones((16,), jnp.float32), (32, 64))
        _ctx_1024t = jnp.einsum('bsk,bkd->bsd', _ctx_1024c, _ctx_1024P)
        _ctx_1024t = _ctx_1024t * jax.lax.rsqrt(jnp.mean(jnp.square(_ctx_1024t)) + 1e-12) * 0.953939
        ctx_1024 = -1.39393e-06 + 0.999914 * (_ctx_1024t + 0.3 * jax.random.normal(jax.random.fold_in(_rk, 611), (32, 64, 128), jnp.float32))
        return (x, ctx_1024)
    x, ctx_1024 = _rec_inputs()

    def _L0_attn_setup():
        import jax, jax.numpy as jnp
        import numpy as np
        D_MODEL = 512
        NUM_HEADS = 32
        HEAD_DIM = D_MODEL // NUM_HEADS
        Q_LAT = 12
        KV_LAT = 4
        B, S = (2, 256)
        key = jax.random.key(seed)
        ks = jax.random.split(key, 6)
        sc = lambda fan_in: 1.0 / np.sqrt(fan_in)
        return {'x': jax.random.normal(ks[0], (B, S, D_MODEL), jnp.float32), 'Wq_d': jax.random.normal(ks[1], (D_MODEL, Q_LAT), jnp.float32) * sc(D_MODEL), 'bq_d': jnp.zeros((Q_LAT,), jnp.float32), 'W_qk': jax.random.normal(ks[2], (Q_LAT, NUM_HEADS * KV_LAT), jnp.float32) * sc(Q_LAT), 'b_qk': jnp.zeros((NUM_HEADS * KV_LAT,), jnp.float32), 'Wkv_d': jax.random.normal(ks[3], (D_MODEL, KV_LAT), jnp.float32) * sc(D_MODEL), 'bkv_d': jnp.zeros((KV_LAT,), jnp.float32), 'Wv_u': jax.random.normal(ks[4], (KV_LAT, NUM_HEADS * HEAD_DIM), jnp.float32) * sc(KV_LAT), 'bv_u': jnp.zeros((NUM_HEADS * HEAD_DIM,), jnp.float32), 'Wo': jax.random.normal(ks[5], (NUM_HEADS * HEAD_DIM, D_MODEL), jnp.float32) * sc(NUM_HEADS * HEAD_DIM), 'bo': jnp.zeros((D_MODEL,), jnp.float32)}
    _L0_attn_all = _L0_attn_setup()
    _L0_attn_in = {k: v for k, v in _L0_attn_all.items() if k in ('Wq_d', 'bq_d', 'W_qk', 'b_qk', 'Wkv_d', 'bkv_d', 'Wv_u', 'bv_u', 'Wo', 'bo')}
    del _L0_attn_all

    def _L0_xattn_setup():
        import jax, jax.numpy as jnp
        import numpy as np
        import math
        DIM_V = 64
        key = jax.random.key(seed)
        k1, k2, k3, k4, k5, k6 = jax.random.split(key, 6)
        B, C, N, M = (8, DIM_V, 512, 128)
        pcd_up = jax.random.normal(k1, (B, C, N), dtype=jnp.float32)
        pcd_down = jax.random.normal(k2, (B, C, M), dtype=jnp.float32)
        s = 1.0 / math.sqrt(C)
        Wq = jax.random.normal(k3, (C, C), dtype=jnp.float32) * s
        Wk = jax.random.normal(k4, (C, C), dtype=jnp.float32) * s
        Wv = jax.random.normal(k5, (C, C), dtype=jnp.float32) * s
        Wskip = jax.random.normal(k6, (C, C), dtype=jnp.float32) * s
        return {'pcd_up': pcd_up, 'pcd_down': pcd_down, 'Wq': Wq, 'Wk': Wk, 'Wv': Wv, 'Wskip': Wskip}
    _L0_xattn_all = _L0_xattn_setup()
    _L0_xattn_in = {k: v for k, v in _L0_xattn_all.items() if k in ('Wq', 'Wk', 'Wv', 'Wskip')}
    del _L0_xattn_all

    def _L0_ffn_setup():
        import jax, jax.numpy as jnp
        import numpy as np
        B_, S, D_IN, D_OUT = (4, 256, 512, 512)
        N, RANK, ALPHA = (8, 16, 32)
        SCALE = ALPHA / RANK
        key = jax.random.key(seed)
        kx, ka, kb, kw, kbias = jax.random.split(key, 5)
        x = jax.random.normal(kx, (B_, S, D_IN), dtype=jnp.float32)
        lora_A = jax.random.normal(ka, (N, RANK, D_IN), dtype=jnp.float32) * (1.0 / np.sqrt(D_IN))
        lora_B = jax.random.normal(kb, (N, D_OUT, RANK), dtype=jnp.float32) * (1.0 / np.sqrt(RANK))
        W = jax.random.normal(kw, (D_OUT, D_IN), dtype=jnp.float32) * (1.0 / np.sqrt(D_IN))
        bias = jax.random.normal(kbias, (D_OUT,), dtype=jnp.float32) * 0.01
        lora_weights = jnp.full((N,), 1.0 / N, dtype=jnp.float32)
        return {'x': x, 'lora_A': lora_A, 'lora_B': lora_B, 'W': W, 'bias': bias, 'lora_weights': lora_weights}
    _L0_ffn_all = _L0_ffn_setup()
    _L0_ffn_in = {k: v for k, v in _L0_ffn_all.items() if k in ('lora_A', 'lora_B', 'W', 'bias', 'lora_weights')}
    del _L0_ffn_all
    return {'x': x, 'ctx_1024': ctx_1024, 'L0_attn_Wq_d': _L0_attn_in['Wq_d'], 'L0_attn_bq_d': _L0_attn_in['bq_d'], 'L0_attn_W_qk': _L0_attn_in['W_qk'], 'L0_attn_b_qk': _L0_attn_in['b_qk'], 'L0_attn_Wkv_d': _L0_attn_in['Wkv_d'], 'L0_attn_bkv_d': _L0_attn_in['bkv_d'], 'L0_attn_Wv_u': _L0_attn_in['Wv_u'], 'L0_attn_bv_u': _L0_attn_in['bv_u'], 'L0_attn_Wo': _L0_attn_in['Wo'], 'L0_attn_bo': _L0_attn_in['bo'], 'L0_xattn_Wq': _L0_xattn_in['Wq'], 'L0_xattn_Wk': _L0_xattn_in['Wk'], 'L0_xattn_Wv': _L0_xattn_in['Wv'], 'L0_xattn_Wskip': _L0_xattn_in['Wskip'], 'L0_ffn_lora_A': _L0_ffn_in['lora_A'], 'L0_ffn_lora_B': _L0_ffn_in['lora_B'], 'L0_ffn_W': _L0_ffn_in['W'], 'L0_ffn_bias': _L0_ffn_in['bias'], 'L0_ffn_lora_weights': _L0_ffn_in['lora_weights']}

def reference(x, ctx_1024, L0_attn_Wq_d, L0_attn_bq_d, L0_attn_W_qk, L0_attn_b_qk, L0_attn_Wkv_d, L0_attn_bkv_d, L0_attn_Wv_u, L0_attn_bv_u, L0_attn_Wo, L0_attn_bo, L0_xattn_Wq, L0_xattn_Wk, L0_xattn_Wv, L0_xattn_Wskip, L0_ffn_lora_A, L0_ffn_lora_B, L0_ffn_W, L0_ffn_bias, L0_ffn_lora_weights):
    import jax
    import jax.numpy as jnp

    def _L0_attn_ref(x, Wq_d, bq_d, W_qk, b_qk, Wkv_d, bkv_d, Wv_u, bv_u, Wo, bo):
        import jax, jax.numpy as jnp
        import numpy as np
        D_MODEL = 512
        NUM_HEADS = 32
        HEAD_DIM = D_MODEL // NUM_HEADS
        Q_LAT = 12
        KV_LAT = 4
        B, S = (2, 256)
        b, s, _ = x.shape
        C_q = x @ Wq_d + bq_d
        C_kv = x @ Wkv_d + bkv_d
        q = (C_q @ W_qk + b_qk).reshape(b, s, NUM_HEADS, KV_LAT)
        scores = jnp.einsum('bqhd,bkd->bhqk', q, C_kv) / jnp.sqrt(jnp.asarray(KV_LAT, x.dtype))
        attn = jax.nn.softmax(scores, axis=-1)
        V = (C_kv @ Wv_u + bv_u).reshape(b, s, NUM_HEADS, HEAD_DIM)
        out = jnp.einsum('bhqk,bkhd->bqhd', attn, V).reshape(b, s, NUM_HEADS * HEAD_DIM)
        return out @ Wo + bo

    def _L0_xattn_ref(pcd_up, pcd_down, Wq, Wk, Wv, Wskip):
        import jax, jax.numpy as jnp
        import numpy as np
        import math
        DIM_V = 64
        q = jnp.einsum('oc,bcn->bon', Wq, pcd_up)
        k = jnp.einsum('oc,bcm->bom', Wk, pcd_down)
        v = jnp.einsum('oc,bcm->bom', Wv, pcd_down)
        C = q.shape[1]
        scale = jnp.sqrt(jnp.asarray(C, dtype=q.dtype))
        energy = jnp.einsum('bcn,bcm->bnm', q, k) / scale
        attention = jax.nn.softmax(energy, axis=-1)
        x = jnp.einsum('bnm,bcm->bcn', attention, v)
        skip = jnp.einsum('oc,bcn->bon', Wskip, pcd_up)
        return skip + x

    def _L0_ffn_ref(x, lora_A, lora_B, W, bias, lora_weights):
        import jax, jax.numpy as jnp
        import numpy as np
        B_, S, D_IN, D_OUT = (4, 256, 512, 512)
        N, RANK, ALPHA = (8, 16, 32)
        SCALE = ALPHA / RANK
        h = jnp.einsum('bsd,nrd->nbsr', x, lora_A)
        coef = (SCALE * lora_weights)[:, None, None]
        lora_out = jnp.einsum('nbsr,nor->bso', h, lora_B * coef)
        base = jnp.einsum('bsd,od->bso', x, W) + bias
        return base + lora_out
    x = x + _L0_attn_ref(_layernorm(x, axis=-1), L0_attn_Wq_d, L0_attn_bq_d, L0_attn_W_qk, L0_attn_b_qk, L0_attn_Wkv_d, L0_attn_bkv_d, L0_attn_Wv_u, L0_attn_bv_u, L0_attn_Wo, L0_attn_bo)
    x = x + _L0_xattn_ref(_layernorm(x, axis=-1), ctx_1024, L0_xattn_Wq, L0_xattn_Wk, L0_xattn_Wv, L0_xattn_Wskip)
    x = x + _L0_ffn_ref(_layernorm(x, axis=-1), L0_ffn_lora_A, L0_ffn_lora_B, L0_ffn_W, L0_ffn_bias, L0_ffn_lora_weights)
    return x

_drawn_inputs = setup_inputs


def setup_inputs(seed=0):
    import zlib

    import numpy as np

    out = dict(_drawn_inputs(seed))
    spreads = {'L0_attn_bq_d': (0.0, 0.1),
     'L0_attn_b_qk': (0.0, 0.1),
     'L0_attn_bkv_d': (0.0, 0.1),
     'L0_attn_bv_u': (0.0, 0.1),
     'L0_attn_bo': (0.0, 0.1),
     'L0_ffn_lora_weights': (0.125, 0.2)}
    factors = {'L0_ffn_bias': 8.0}
    for name, (base, spread) in spreads.items():
        noise = np.random.default_rng([zlib.crc32(name.encode()), seed]).standard_normal(out[name].shape)
        drawn = base * np.exp(spread * noise) if base else spread * noise
        out[name] = jnp.asarray(drawn.astype(out[name].dtype))
    for name, factor in factors.items():
        out[name] = (out[name] * factor).astype(out[name].dtype)
    return out
```

```python
from contextlib import ExitStack

import concourse.bass as bass
from concourse import mybir

F32 = mybir.dt.float32
BF16 = mybir.dt.bfloat16
ALU = mybir.AluOpType
ACT = mybir.ActivationFunctionType
AX_X = mybir.AxisListType.X

P = 128
B, S, D = 32, 64, 512
PAIRS = B * S // P
DC = D // P
H, LAT, QL = 32, 4, 12
HP = H // 2
HD = D // H
CD, CM = S, P
NL, RANK, ALPHA = 8, 16, 32
EPS = 1e-5
NPART = 3
KROWS = NPART * NPART * LAT
KALL = KROWS + NPART
WIDE = 2 * 512


def done(n, u, back=0):
    return 2 * n + (u + 1 - back)


def decoder(nc, io):
    x_d = io["x"].rearrange("b s d -> (b s) d")
    ctx_d = io["ctx_1024"].rearrange("b c m -> (b c) m")
    out_d = io["out"].rearrange("b s d -> (b s) d")
    es = ExitStack()
    with es:
        def sb(name, shape, dt=F32):
            return es.enter_context(nc.sbuf_tensor(name, shape, dt))

        def sem(name):
            return es.enter_context(nc.semaphore(name))

        identf = sb("identf", [P, P])
        ident = sb("ident", [P, P], BF16)
        negid = sb("negid", [P, P], BF16)
        half36 = sb("half36", [P, 2, KROWS], BF16)
        half5 = sb("half5", [P, 2, LAT + 1])
        mhalf = sb("mhalf", [P, 1])
        epsc = sb("epsc", [P, 1])
        ones = sb("ones", [P, P])
        meanw = sb("meanw", [P, P])
        wqd = sb("wqd", [P, DC, QL])
        w13 = sb("w13", [QL + 1, P])
        w13p = sb("w13p", [QL + 1, P])
        bq13 = sb("bq13", [QL + 1, 1])
        wqdT = sb("wqdT", [QL, D])
        wqc = sb("wqc", [P, DC, P])
        bqc = sb("bqc", [P, 1])
        wkv = sb("wkv", [P, DC, LAT])
        bkv = sb("bkv", [P, LAT])
        wvu = sb("wvu", [LAT, D])
        vT = sb("vT", [P, DC * LAT + DC])
        wvuT = vT[:, 0:DC * LAT].rearrange("p (c j) -> p c j", j=LAT)
        hmask = sb("hmask", [P, DC, H])
        vbd = sb("vbd", [P, DC, H, LAT])
        wo = sb("wo", [P, DC, D])
        bvr = sb("bvr", [DC, P])
        bvT = vT[:, DC * LAT:DC * LAT + DC]
        bo = sb("bo", [P, D])
        mout = sb("mout", [P, D])
        cvec = sb("cvec", [P, D])
        xwk = sb("xwk", [CD, 2, CD])
        xwq = sb("xwq", [CD, CD])
        xwv = sb("xwv", [CD, 2, CD])
        xws = sb("xws", [CD, 2, CD])
        kq = sb("kq", [P, P])
        wvbd = sb("wvbd", [P, P])
        wsbd = sb("wsbd", [P, P])
        fw = sb("fw", [P, DC, D])
        la = sb("la", [P, D])
        lb = sb("lb", [P, DC, NL, RANK])
        lbT = sb("lbT", [P, D])
        lw = sb("lw", [NL, 1])
        spread = sb("spread", [NL, P])
        coef = sb("coef", [P, 1])
        weff = sb("weff", [P, DC, D])
        fbias = sb("fbias", [P, D])

        def two(name, shape, dt=F32):
            return [sb(f"{name}{u}", shape, dt) for u in range(2)]

        xin = two("xin", [P, D])
        st1 = sb("st1", [P, 6])
        mv1 = sb("mv1", [P, 2])
        rs1 = sb("rs1", [P, 2])
        xn = two("xn", [P, D])
        x0b = two("x0b", [P, D])
        xnT = sb("xnT", [P, DC, P])
        q32 = sb("q32", [P, P])
        qr = sb("qr", [P, 2, S])
        qpart = two("qpart", [P, 2, NPART, S], BF16)
        c32 = sb("c32", [P, LAT])
        c5 = sb("c5", [P, LAT + 1])
        cr = sb("cr", [P, LAT])
        cs = sb("cs", [P, NPART, NPART, LAT], BF16)
        ctile = two("ctile", [P, 2, S], BF16)
        cbd = two("cbd", [P, 2, LAT + 1])
        cst = two("cst", [P, P], BF16)
        qst = two("qst", [P, H * S], BF16)
        mx0 = two("mx0", [P, 2, HP])
        mr0 = sb("mr0", [P, 2, HP])
        mp0 = sb("mp0", [P, 2, NPART, HP], BF16)
        mx0T = two("mx0T", [2 * NPART * HP, P], BF16)
        p0 = sb("p0", [P, H * S])
        rden0 = sb("rden0", [P, 2, HP])
        ctxn = sb("ctxn", [P, 2, HP, LAT])
        ctxT = sb("ctxT", [P, P])
        x1 = sb("x1", [P, D])
        st2 = sb("st2", [P, 6])
        mv2 = two("mv2", [P, 2])
        ve2 = sb("ve2", [P, 1])
        rs2 = two("rs2", [P, 1])
        x1c = two("x1c", [P, D])
        cin = two("cin", [P, CM])
        g = sb("g", [P, CM])
        v65 = two("v65", [P, 2, CD + 1])
        mx1 = sb("mx1", [P, 2, DC])
        mr1 = sb("mr1", [P, 2, DC])
        mp1 = sb("mp1", [P, NPART, 2, DC], BF16)
        pt = sb("pt", [P, 2, D])
        rmat = sb("rmat", [P, P])
        rden1 = sb("rden1", [P, 2, DC])
        pvn = sb("pvn", [P, DC, 2, CD])
        x2T = two("x2T", [P, DC, P])
        st3 = sb("st3", [P, 6])
        mv3 = sb("mv3", [P, 2])
        ve3 = sb("ve3", [P, 1])
        rs3 = sb("rs3", [P, 1])
        x2s = sb("x2s", [P, D])
        x2b = sb("x2b", [P, D])
        y = two("y", [P, D])

        q_scr = [nc.dram_tensor(f"q_scr{u}", (2 * NPART, P, S), BF16, kind="Internal").ap() for u in range(2)]
        m_scr = [nc.dram_tensor(f"m_scr{u}", (2 * NPART * HP, P), BF16, kind="Internal").ap() for u in range(2)]

        W = [es.enter_context(nc.psum_tensor(f"wide{k}", [P, WIDE], F32)) for k in range(2)]
        M = [es.enter_context(nc.psum_tensor(f"bank{k}", [P, 512], F32)) for k in range(4)]

        names = """ld_attn ld_vo ld_x ld_ffn prep_pool wqdT_ps wvuT_ps cols_ps wqc_ps xw_ps lbT_ps mout_ps w13p halves cvec_ps wT_ps lora_ps wmean_ps wqdT wvuT coef wqc xw mout wT vbd lbT cvec weff wcen
        st1 mv1 ve1 rs1 xn xT xnT x0b qc q32 qh c32 qr qm ql c5 ch cr cm cl cbd ctile cstT cst
        a0_0 a0_1 mx0_0 mx0_1 mh0 mr0 mm0 ml0 mT0 mx0T b0_0 b0_1 e0_0 e0_1 pv0 rden0 ctxn ctxTa ctxTb ctx_lo ctx_hi
        o x1 st2 mv2 ve2 rs2 x1c gv g v xa mx1 mh1 mr1 mm1 ml1 xb e1 rmat skip pv1 rden1 pvn x2T
        x2 st3 mv3 ve3 rs3 x2s ffn x2b y"""
        s = {n: sem("s_" + n) for n in names.split()}
        ld_x = [sem(f"s_xin{u}") for u in range(2)]
        ld_c = [sem(f"s_cin{u}") for u in range(2)]
        q_out = [sem(f"s_qout{u}") for u in range(2)]
        q_in = [sem(f"s_qin{u}") for u in range(2)]
        m_out = [sem(f"s_mout{u}") for u in range(2)]
        m_in = [sem(f"s_min{u}") for u in range(2)]
        y_out = [sem(f"s_stored{u}") for u in range(2)]

        steps = PAIRS + 4

        def run(eng, step):
            def pairs(i):
                return [(i - k) // 2 if 0 <= i - k < PAIRS else None for k in range(5)]
            for i in range(6):
                step(i % 2, pairs(i))
            with eng.Fori(3, PAIRS // 2) as j:
                for r in range(2):
                    step(r, [j + (r - k) // 2 if (r - k) // 2 else j for k in range(5)])
            for i in range(PAIRS, steps):
                step(i % 2, pairs(i))

        def has(n, u, back):
            return not isinstance(n, int) or 2 * n + u >= back

        def last(n, u):
            return isinstance(n, int) and 2 * n + u == PAIRS - 1

        def nth(n, k):
            return n * (16 * k) + 16 * k

        block = es.enter_context(nc.Block())

        @block.sync
        def _(sp):
            sp.dma_start(wqd[:], io["L0_attn_Wq_d"].rearrange("(c p) k -> p c k", p=P)).then_inc(s["ld_attn"], 16)
            sp.dma_start(w13[0:QL, :], io["L0_attn_W_qk"]).then_inc(s["ld_attn"], 16)
            sp.dma_start(w13[QL:QL + 1, :], io["L0_attn_b_qk"].rearrange("(a n) -> a n", a=1)).then_inc(s["ld_attn"], 16)
            sp.wait_ge(s["prep_pool"], 1)
            sp.dma_start(bq13[0:QL, :], io["L0_attn_bq_d"].rearrange("(n a) -> n a", a=1)).then_inc(s["ld_attn"], 16)
            sp.dma_start(wkv[:], io["L0_attn_Wkv_d"].rearrange("(c p) k -> p c k", p=P)).then_inc(s["ld_attn"], 16)
            sp.dma_start(bkv[:], io["L0_attn_bkv_d"].rearrange("(a n) -> a n", a=1).broadcast_to([P, LAT])).then_inc(s["ld_attn"], 16)

            def step(r, n):
                def p1_load(n, u):
                    if has(n, u, 2):
                        sp.wait_ge(s["xn"], done(n, u, 2))
                        sp.nop(nofuse=True)
                        sp.wait_ge(s["x0b"], done(n, u, 2))
                        sp.nop(nofuse=True)
                    sp.dma_start(xin[u][:], x_d[bass.ds((n * 2 + u) * P, P), :]).then_inc(ld_x[u], 16)

                def p2_max(n, u):
                    sp.wait_ge(s["mx0T"], done(n, u))
                    sp.nop(nofuse=True)
                    sp.dma_start(m_scr[u], mx0T[u][:]).then_inc(m_out[u], 16)
                    sp.wait_ge(m_out[u], nth(n, 1))
                    sp.nop(nofuse=True)
                    for b in range(2):
                        sp.dma_start(qst[u][64 * b + KROWS:64 * b + KALL, :],
                                     m_scr[u].rearrange("(b a h) q -> b a (h q)", b=2, a=NPART)[b]).then_inc(m_in[u], 16)

                def p1_q(n, u):
                    if has(n, u, 2):
                        sp.wait_ge(q_in[u], nth(n - 1, 6))
                        sp.nop(nofuse=True)
                    sp.wait_ge(s["ql"], done(n, u))
                    sp.nop(nofuse=True)
                    sp.dma_start(q_scr[u].rearrange("k p q -> p k q"),
                                 qpart[u][:].rearrange("p b a q -> p (b a) q")).then_inc(q_out[u], 16)
                    sp.wait_ge(q_out[u], nth(n, 1))
                    sp.nop(nofuse=True)
                    if has(n, u, 2):
                        sp.wait_ge(s["b0_1"], done(n, u, 2))
                        sp.nop(nofuse=True)
                    for b in range(2):
                        rows = q_scr[u][NPART * b:NPART * (b + 1)].rearrange("a (j h) q -> (a j) (h q)", j=LAT)
                        for part in range(NPART):
                            r0 = 64 * b + part * NPART * LAT
                            sp.dma_start(qst[u][r0:r0 + NPART * LAT, :], rows).then_inc(q_in[u], 16)

                def p4_load(n, u):
                    if has(n, u, 2):
                        sp.wait_ge(s["gv"], done(n, u, 2))
                        sp.nop(nofuse=True)
                    sp.dma_start(cin[u][:], ctx_d[bass.ds((n * 2 + u) * P, P), :]).then_inc(ld_c[u], 16)

                def p5_store(n, u):
                    sp.wait_ge(s["y"], done(n, u))
                    sp.nop(nofuse=True)
                    sp.dma_start(out_d[bass.ds((n * 2 + u) * P, P), :], y[u][:]).then_inc(y_out[u], 16)

                if n[0] is not None:
                    p1_load(n[0], r)
                if n[2] is not None:
                    p4_load(n[2], r)
                if n[1] is not None:
                    p2_max(n[1], 1 - r)
                if n[0] is not None:
                    p1_q(n[0], r)
                if n[4] is not None:
                    p5_store(n[4], r)

            run(sp, step)
            for u in range(2):
                sp.wait_ge(y_out[u], nth(PAIRS // 2 - 1, 1))

        @block.gpsimd
        def _(pool):
            nc.gpsimd.memset(bq13[:], 1.0).then_inc(s["prep_pool"], 1)
            nc.gpsimd.memset(identf[:], 0.0)
            nc.gpsimd.memset(mhalf[:], -0.5)
            nc.gpsimd.memset(epsc[:], EPS)
            nc.gpsimd.memset(ones[:], 1.0)
            nc.gpsimd.memset(meanw[:], 1.0 / D)
            nc.gpsimd.memset(c5[:], 1.0)
            for t_ in (half36, half5, kq, wvbd, wsbd):
                nc.gpsimd.memset(t_[:], 0.0)
            nc.gpsimd.memset(spread[:], 1.0)
            for u in range(2):
                nc.gpsimd.memset(ctile[u][:], 0.0)
                nc.gpsimd.memset(qst[u][:], 0.0)
                nc.gpsimd.memset(v65[u][:], 1.0)
            nc.gpsimd.memset(hmask[:], 1.0).then_inc(s["prep_pool"], 1)
            pool.wait_ge(s["prep_pool"], 2)
            nc.gpsimd.affine_select(out=hmask[:], in_=hmask[:], compare_op=ALU.is_ge, fill=0.0, base=0,
                                    pattern=[[P, DC], [-HD, 2], [-2 * HD, HP]], channel_multiplier=1)
            nc.gpsimd.affine_select(out=spread[:], in_=spread[:], compare_op=ALU.is_ge, fill=0.0, base=0,
                                    pattern=[[1, P]], channel_multiplier=-RANK)
            nc.gpsimd.affine_select(out=identf[:], in_=identf[:], compare_op=ALU.not_equal, fill=1.0, base=0,
                                    pattern=[[-1, P]], channel_multiplier=1).then_inc(s["prep_pool"], 1)
            pool.wait_ge(s["prep_pool"], 3)
            nc.gpsimd.affine_select(out=hmask[:], in_=hmask[:], compare_op=ALU.is_ge, fill=0.0, base=HD - 1,
                                    pattern=[[-P, DC], [HD, 2], [2 * HD, HP]], channel_multiplier=-1)
            nc.gpsimd.affine_select(out=spread[:], in_=spread[:], compare_op=ALU.is_ge, fill=0.0, base=RANK - 1,
                                    pattern=[[-1, P]], channel_multiplier=RANK)
            nc.gpsimd.tensor_copy(ident[:], identf[:])
            nc.gpsimd.tensor_scalar(negid[:], identf[:], -1.0, 0.0, ALU.mult, ALU.add).then_inc(s["prep_pool"], 1)

            pool.wait_ge(s["ld_attn"], 96)
            nc.gpsimd.tensor_copy(w13p[:].rearrange("c (j h) -> c j h", j=LAT),
                                  w13[:].rearrange("c (h j) -> c j h", j=LAT)).then_inc(s["w13p"], 1)

            def rstd(ve, var, out, wait_var, ve_done, rs_done, n, u):
                pool.wait_ge(s[wait_var], done(n, u))
                nc.gpsimd.tensor_tensor(ve, var, epsc[:], ALU.add).then_inc(s[ve_done], 1)
                pool.wait_ge(s[ve_done], done(n, u))
                nc.gpsimd.tensor_tensor(out, ve, mhalf[:], ALU.pow).then_inc(s[rs_done], 1)

            def step(r, n):
                def p1_rstd(n, u):
                    rstd(rs1[:, 1:2], mv1[:, 1:2], rs1[:, 0:1], "mv1", "ve1", "rs1", n, u)

                def p1_residual(n, u):
                    if not has(n, u, 1):
                        pool.wait_ge(s["cvec"], 1)
                    if has(n, u, 2):
                        pool.wait_ge(s["x1"], done(n, u, 2))
                    pool.wait_ge(ld_x[u], nth(n, 1))
                    nc.gpsimd.tensor_tensor(x0b[u][:], xin[u][:], cvec[:], ALU.add).then_inc(s["x0b"], 1)

                def p1_q(n, u):
                    pool.wait_ge(s["qh"], done(n, u))
                    nc.gpsimd.tensor_tensor(qr[:], q32[:].rearrange("p (b q) -> p b q", b=2), qpart[u][:, :, 0, :], ALU.subtract).then_inc(s["qr"], 1)
                    pool.wait_ge(s["qr"], done(n, u))
                    nc.gpsimd.tensor_tensor(qpart[u][:, :, 1, :], qr[:], ones[:].rearrange("p (b q) -> p b q", b=2), ALU.mult).then_inc(s["qm"], 1)
                    pool.wait_ge(s["qm"], done(n, u))
                    nc.gpsimd.tensor_tensor(qpart[u][:, :, 2, :], qr[:], qpart[u][:, :, 1, :], ALU.subtract).then_inc(s["ql"], 1)

                def p1_c(n, u):
                    pool.wait_ge(s["c32"], done(n, u))
                    nc.gpsimd.tensor_tensor(c5[:, 0:LAT], c32[:], bkv[:], ALU.add).then_inc(s["c5"], 1)
                    pool.wait_ge(s["c5"], done(n, u))
                    c_all = c5[:, 0:LAT].unsqueeze(1).broadcast_to([P, NPART, LAT])
                    r_all = cr[:].unsqueeze(1).broadcast_to([P, NPART, LAT])
                    ones12 = ones[:, 0:NPART * LAT].rearrange("p (a j) -> p a j", j=LAT)
                    nc.gpsimd.tensor_tensor(cs[:, 0], c_all, ones12, ALU.mult).then_inc(s["ch"], 1)
                    if has(n, u, 2):
                        pool.wait_ge(s["pv0"], done(n, u, 2))
                    nc.gpsimd.tensor_tensor(cbd[u][:], c5[:].unsqueeze(1).broadcast_to([P, 2, LAT + 1]),
                                            half5[:], ALU.mult).then_inc(s["cbd"], 1)
                    pool.wait_ge(s["ch"], done(n, u))
                    nc.gpsimd.tensor_tensor(cr[:], c5[:, 0:LAT], cs[:, 0, 0], ALU.subtract).then_inc(s["cr"], 1)
                    pool.wait_ge(s["cr"], done(n, u))
                    nc.gpsimd.tensor_tensor(cs[:, 1], r_all, ones12, ALU.mult).then_inc(s["cm"], 1)
                    pool.wait_ge(s["cm"], done(n, u))
                    nc.gpsimd.tensor_tensor(cs[:, 2], r_all, cs[:, 1], ALU.subtract).then_inc(s["cl"], 1)
                    pool.wait_ge(s["cl"], done(n, u))
                    if has(n, u, 2):
                        pool.wait_ge(s["cstT"], done(n, u, 2))
                    nc.gpsimd.tensor_tensor(ctile[u][:, :, 0:KROWS],
                                            cs[:].rearrange("p b a j -> p (b a j)").unsqueeze(1).broadcast_to([P, 2, KROWS]),
                                            half36[:], ALU.mult).then_inc(s["ctile"], 1)

                def split(x, one, parts, rest, sx, h, mid, rr, low, n, u):
                    for k in sx:
                        pool.wait_ge(s[k], done(n, u))
                    nc.gpsimd.tensor_tensor(parts[0], x, one, ALU.mult).then_inc(s[h], 1)
                    pool.wait_ge(s[h], done(n, u))
                    nc.gpsimd.tensor_tensor(rest, x, parts[0], ALU.subtract).then_inc(s[rr], 1)
                    pool.wait_ge(s[rr], done(n, u))
                    nc.gpsimd.tensor_tensor(parts[1], rest, one, ALU.mult).then_inc(s[mid], 1)
                    pool.wait_ge(s[mid], done(n, u))
                    nc.gpsimd.tensor_tensor(parts[2], rest, parts[1], ALU.subtract).then_inc(s[low], 1)

                def p2_split(n, u):
                    if has(n, u, 1):
                        pool.wait_ge(s["mT0"], done(n, u, 1))
                    split(mx0[u][:], ones[:, 0:2 * HP].rearrange("p (b h) -> p b h", b=2), [mp0[:, :, k, :] for k in range(NPART)], mr0[:],
                          ("mx0_0", "mx0_1"), "mh0", "mm0", "mr0", "ml0", n, u)

                def p3_rstd(n, u):
                    if has(n, u, 2):
                        pool.wait_ge(s["rmat"], done(n, u, 2))
                        pool.wait_ge(s["g"], done(n, u, 2))
                    rstd(ve2[:], mv2[u][:, 1:2], rs2[u][:], "mv2", "ve2", "rs2", n, u)

                def p4_split(n, u):
                    if has(n, u, 1):
                        pool.wait_ge(s["xb"], done(n, u, 1))
                    split(mx1[:], ones[:, 0:2 * DC].rearrange("p (b c) -> p b c", b=2), [mp1[:, k] for k in range(NPART)], mr1[:], ("mx1",), "mh1", "mm1", "mr1", "ml1", n, u)

                def p5_rstd(n, u):
                    if has(n, u, 1):
                        pool.wait_ge(s["y"], done(n, u, 1))
                    rstd(ve3[:], mv3[:, 1:2], rs3[:], "mv3", "ve3", "rs3", n, u)

                def p5_bias(n, u):
                    pool.wait_ge(s["x2s"], done(n, u))
                    if has(n, u, 1):
                        pool.wait_ge(s["y"], done(n, u, 1))
                    nc.gpsimd.tensor_tensor(x2b[:], x2s[:], fbias[:], ALU.add).then_inc(s["x2b"], 1)

                if n[0] is not None:
                    p1_rstd(n[0], r)
                if n[1] is not None:
                    p2_split(n[1], 1 - r)
                if n[4] is not None:
                    p5_rstd(n[4], r)
                    p5_bias(n[4], r)
                if n[0] is not None:
                    p1_q(n[0], r)
                    p1_c(n[0], r)
                if n[3] is not None:
                    p4_split(n[3], 1 - r)
                if n[0] is not None:
                    p1_residual(n[0], r)
                if n[2] is not None:
                    p3_rstd(n[2], r)

            pool.wait_ge(s["halves"], 1)
            pool.wait_ge(s["ld_ffn"], 16 * 8)
            run(pool, step)

        @block.scalar
        def _(act):
            act.dma_start(wvu[:], io["L0_attn_Wv_u"]).then_inc(s["ld_vo"], 16)
            act.dma_start(wo[:], io["L0_attn_Wo"].rearrange("(c p) n -> p c n", p=P)).then_inc(s["ld_vo"], 16)
            act.dma_start(bvr[:], io["L0_attn_bv_u"].rearrange("(c p) -> c p", p=P)).then_inc(s["ld_vo"], 16)
            act.dma_start(bo[:], io["L0_attn_bo"].rearrange("(a n) -> a n", a=1).broadcast_to([P, D])).then_inc(s["ld_vo"], 16)
            act.dma_start(xwq[:], io["L0_xattn_Wq"]).then_inc(s["ld_x"], 16)
            for k in range(2):
                act.dma_start(xwk[:, k, :], io["L0_xattn_Wk"]).then_inc(s["ld_x"], 16)
                act.dma_start(xwv[:, k, :], io["L0_xattn_Wv"]).then_inc(s["ld_x"], 16)
                act.dma_start(xws[:, k, :], io["L0_xattn_Wskip"]).then_inc(s["ld_x"], 16)
            act.dma_start(fw[:], io["L0_ffn_W"].rearrange("(c p) n -> p c n", p=P)).then_inc(s["ld_ffn"], 16)
            act.dma_start(la[:], io["L0_ffn_lora_A"].rearrange("n r d -> (n r) d")).then_inc(s["ld_ffn"], 16)
            for c in range(DC):
                act.dma_start(lb[:, c], io["L0_ffn_lora_B"][:, c * P:(c + 1) * P, :].rearrange("n p r -> p n r")).then_inc(s["ld_ffn"], 16)
            act.dma_start(lw[:], io["L0_ffn_lora_weights"].rearrange("(n a) -> n a", a=1)).then_inc(s["ld_ffn"], 16)
            act.dma_start(fbias[:], io["L0_ffn_bias"].rearrange("(a n) -> a n", a=1).broadcast_to([P, D])).then_inc(s["ld_ffn"], 16)

            act.wait_ge(s["wqdT_ps"], 1)
            nc.scalar.copy(wqdT[:], M[0][0:QL, :]).then_inc(s["wqdT"], 1)
            act.wait_ge(s["cols_ps"], 1)
            nc.scalar.copy(vT[:], M[1][:, 0:DC * LAT + DC]).then_inc(s["wvuT"], 1)
            nc.scalar.copy(bqc[:], M[1][:, 32:33])
            nc.scalar.mul(coef[:], M[1][:, 33:34], float(ALPHA) / RANK).then_inc(s["coef"], 1)
            act.wait_ge(s["wqc_ps"], 1)
            nc.scalar.copy(wqc[:].rearrange("p c n -> p (c n)"), M[0][:]).then_inc(s["wqc"], 1)
            act.wait_ge(s["xw_ps"], 1)
            for b in range(2):
                q_ = slice(64 * b, 64 * b + 64)
                nc.scalar.copy(kq[q_, q_], M[2][q_, 0:64])
                nc.scalar.copy(wvbd[q_, q_], M[2][q_, 64:128])
                fin = nc.scalar.copy(wsbd[q_, q_], M[2][q_, 128:192])
            fin.then_inc(s["xw"], 1)
            act.wait_ge(s["mout_ps"], 1)
            nc.scalar.copy(mout[:], M[3][:]).then_inc(s["mout"], 1)
            for k in range(DC):
                act.wait_ge(s["wT_ps"], k + 1)
                nc.scalar.copy(weff[:, k], W[k // 2][:, (k % 2) * 512:(k % 2) * 512 + 512]).then_inc(s["wT"], 1)

            def step(r, n):
                def p1_xT(n, u):
                    act.wait_ge(s["xT"], done(n, u))
                    if has(n, u, 1):
                        act.wait_ge(s["qc"], done(n, u, 1))
                    nc.scalar.copy(xnT[:].rearrange("p c t -> p (c t)"), M[0][:]).then_inc(s["xnT"], 1)

                def p1_q(n, u):
                    act.wait_ge(s["qc"], done(n, u))
                    if has(n, u, 1):
                        act.wait_ge(s["qr"], done(n, u, 1))
                        act.wait_ge(s["c5"], done(n, u, 1))
                    nc.scalar.activation(q32[:], M[0][:, 0:P], ACT.Identity, bias=bqc[:]).then_inc(s["q32"], 1)
                    if has(n, u, 2):
                        act.wait_ge(q_out[u], nth(n - 1, 1))
                    nc.scalar.activation(qpart[u][:, :, 0, :], M[0][:, 0:P].rearrange("p (b q) -> p b q", b=2), ACT.Identity, bias=bqc[:]).then_inc(s["qh"], 1)
                    nc.scalar.copy(c32[:], M[0][:, P:P + LAT]).then_inc(s["c32"], 1)

                def p1_c(n, u):
                    act.wait_ge(s["cstT"], done(n, u))
                    if has(n, u, 2):
                        act.wait_ge(s["b0_1"], done(n, u, 2))
                    nc.scalar.copy(cst[u][:], M[0][:].bitcast(BF16)[:, 0:P]).then_inc(s["cst"], 1)

                def p2_max(n, u):
                    act.wait_ge(s["mT0"], done(n, u))
                    if has(n, u, 2):
                        act.wait_ge(m_out[u], nth(n - 1, 1))
                    nc.scalar.copy(mx0T[u][:], M[1][:].bitcast(BF16)[0:2 * NPART * HP, 0:P]).then_inc(s["mx0T"], 1)

                def p3_exp(n, u, k):
                    act.wait_ge(s[f"b0_{k}"], done(n, u))
                    if has(n, u, 1):
                        act.wait_ge(s["pv0"], done(n, u, 1))
                    nc.scalar.activation(p0[:, k * WIDE:(k + 1) * WIDE], W[k][:], ACT.Exp,
                                         scale=float(LAT) ** -0.5).then_inc(s[f"e0_{k}"], 1)

                def p3_ctx(n, u):
                    act.wait_ge(s["ctxTb"], done(n, u))
                    if has(n, u, 1):
                        act.wait_ge(s["o"], done(n, u, 1))
                    nc.scalar.copy(ctxT[0:64, :], M[1][0:64, 0:P]).then_inc(s["ctx_lo"], 1)
                    nc.scalar.copy(ctxT[64:128, :], M[2][64:128, 0:P]).then_inc(s["ctx_hi"], 1)

                def p4_gv(n, u):
                    act.wait_ge(s["gv"], done(n, u))
                    act.wait_ge(s["rs2"], done(n, u))
                    if has(n, u, 1):
                        act.wait_ge(s["xb"], done(n, u, 1))
                    nc.scalar.activation(g[:], M[2][:, 0:CM], ACT.Copy, scale=rs2[u][:]).then_inc(s["g"], 1)
                    if has(n, u, 2):
                        act.wait_ge(s["pv1"], done(n, u, 2))
                    nc.scalar.copy(v65[u][:, :, 0:CD], M[2][:, CM:CM + P].rearrange("p (b c) -> p b c", b=2)).then_inc(s["v"], 1)

                def p4_exp(n, u):
                    act.wait_ge(s["xb"], done(n, u))
                    if has(n, u, 1):
                        act.wait_ge(s["pv1"], done(n, u, 1))
                    nc.scalar.activation(pt[:].rearrange("p b n -> p (b n)"), W[1][:], ACT.Exp,
                                         scale=float(CD) ** -0.5).then_inc(s["e1"], 1)

                def p5_x2(n, u):
                    act.wait_ge(s["x2"], done(n, u))
                    act.wait_ge(s["st3"], done(n, u))
                    if has(n, u, 1):
                        act.wait_ge(s["x2b"], done(n, u, 1))
                    nc.scalar.activation(x2s[:], M[3][:], ACT.Identity, bias=mv2[u][:, 0:1]).then_inc(s["x2s"], 1)

                if n[3] is not None:
                    p4_gv(n[3], 1 - r)
                if n[0] is not None:
                    p1_xT(n[0], r)
                if n[4] is not None:
                    p5_x2(n[4], r)
                if n[2] is not None:
                    p3_exp(n[2], r, 0)
                if n[0] is not None:
                    p1_q(n[0], r)
                if n[2] is not None:
                    p3_exp(n[2], r, 1)
                if n[1] is not None:
                    p2_max(n[1], 1 - r)
                if n[0] is not None:
                    p1_c(n[0], r)
                if n[2] is not None:
                    p3_ctx(n[2], r)
                if n[3] is not None:
                    p4_exp(n[3], 1 - r)

            run(act, step)

        @block.vector
        def _(dve):
            dve.wait_ge(s["prep_pool"], 2)
            for b in range(2):
                nc.vector.memset(half36[64 * b:64 * b + 64, b, :], 1.0)
                nc.vector.memset(half5[64 * b:64 * b + 64, b, :], 1.0)
                for u in range(2):
                    ins = nc.vector.memset(ctile[u][64 * b:64 * b + 64, b, KROWS:KALL], -1.0)
            ins.then_inc(s["halves"], 1)
            dve.wait_ge(s["wvuT"], 1)
            dve.wait_ge(s["prep_pool"], 4)
            for c in range(DC):
                ins = nc.vector.tensor_tensor(vbd[:, c], hmask[:, c].unsqueeze(2).broadcast_to([P, H, LAT]),
                                              wvuT[:, c].unsqueeze(1).broadcast_to([P, H, LAT]), ALU.mult)
            ins.then_inc(s["vbd"], 1)
            dve.wait_ge(s["coef"], 1)
            dve.wait_ge(s["lbT_ps"], 1)
            nc.vector.tensor_scalar(lbT[:], W[0][:, 0:D], coef[:], None, ALU.mult).then_inc(s["lbT"], 1)
            dve.wait_ge(s["cvec_ps"], 1)
            nc.vector.tensor_tensor(cvec[:], W[0][:, 512:1024], bo[:], ALU.add).then_inc(s["cvec"], 1)
            for k in range(DC):
                dve.wait_ge(s["lora_ps"], k + 1)
                dve.wait_ge(s["wT"], k + 1)
                nc.vector.tensor_tensor(weff[:, k], M[k % 2][:], weff[:, k], ALU.add).then_inc(s["weff"], 1)
            dve.wait_ge(s["wmean_ps"], 1)
            for k in range(DC):
                nc.vector.tensor_tensor(weff[:, k], weff[:, k], M[2][:], ALU.subtract).then_inc(s["wcen"], 1)

            def step(r, n):
                def p1_norm(n, u):
                    dve.wait_ge(ld_x[u], nth(n, 1))
                    nc.vector.bn_stats(st1[:], xin[u][:]).then_inc(s["st1"], 1)
                    dve.wait_ge(s["st1"], done(n, u))
                    dve.nop(nofuse=True)
                    nc.vector.bn_aggr(mv1[:], st1[:]).then_inc(s["mv1"], 1)

                def p1_xn(n, u):
                    dve.wait_ge(s["rs1"], done(n, u))
                    if has(n, u, 2):
                        dve.wait_ge(s["xT"], done(n, u, 2))
                    nc.vector.tensor_scalar(xn[u][:], xin[u][:], mv1[:, 0:1], rs1[:, 0:1], ALU.subtract, ALU.mult).then_inc(s["xn"], 1)

                def p2_max(n, u, b):
                    dve.wait_ge(s[f"a0_{b}"], done(n, u))
                    if has(n, u, 2):
                        dve.wait_ge(s["ml0"], done(n, u, 2))
                    nc.vector.tensor_reduce(mx0[u][:, b, :], W[b][:].rearrange("p (h k) -> p h k", k=S), AX_X, ALU.max)\
                        .then_inc(s[f"mx0_{b}"], 1)

                def p3_ctx(n, u):
                    pv = M[1][:, 0:HP * 2 * (LAT + 1)].rearrange("p (h b j) -> p b h j", b=2, j=LAT + 1)
                    dve.wait_ge(s["pv0"], done(n, u))
                    nc.vector.reciprocal(rden0[:], pv[:, :, :, LAT]).then_inc(s["rden0"], 1)
                    dve.wait_ge(s["rden0"], done(n, u))
                    if has(n, u, 1):
                        dve.wait_ge(s["ctxTb"], done(n, u, 1))
                    nc.vector.tensor_tensor(ctxn[:], pv[:, :, :, 0:LAT],
                                            rden0[:].unsqueeze(3).broadcast_to([P, 2, HP, LAT]), ALU.mult).then_inc(s["ctxn"], 1)

                def p3_x1(n, u):
                    dve.wait_ge(s["o"], done(n, u))
                    dve.wait_ge(s["x0b"], done(n, u))
                    nc.vector.tensor_tensor(x1[:], M[2][:], x0b[u][:], ALU.add).then_inc(s["x1"], 1)
                    dve.wait_ge(s["x1"], done(n, u))
                    nc.vector.bn_stats(st2[:], x1[:]).then_inc(s["st2"], 1)
                    dve.wait_ge(s["st2"], done(n, u))
                    if has(n, u, 2):
                        dve.wait_ge(s["x2s"], done(n, u, 2))
                    dve.nop(nofuse=True)
                    nc.vector.bn_aggr(mv2[u][:], st2[:]).then_inc(s["mv2"], 1)
                    dve.wait_ge(s["mv2"], done(n, u))
                    if has(n, u, 2):
                        dve.wait_ge(s["skip"], done(n, u, 2))
                        dve.wait_ge(s["xb"], done(n, u, 2))
                    nc.vector.tensor_scalar(x1c[u][:], x1[:], mv2[u][:, 0:1], None, ALU.subtract).then_inc(s["x1c"], 1)

                def p4_max(n, u):
                    dve.wait_ge(s["xa"], done(n, u))
                    if has(n, u, 1):
                        dve.wait_ge(s["ml1"], done(n, u, 1))
                    nc.vector.tensor_reduce(mx1[:].rearrange("p b c -> p (b c)"), W[0][:].rearrange("p (c m) -> p c m", m=CM),
                                            AX_X, ALU.max).then_inc(s["mx1"], 1)

                def p4_rmat(n, u):
                    dve.wait_ge(s["rs2"], done(n, u))
                    if has(n, u, 1):
                        dve.wait_ge(s["skip"], done(n, u, 1))
                    nc.vector.scalar_tensor_tensor(rmat[:], wsbd[:], rs2[u][:], identf[:], ALU.mult, ALU.add).then_inc(s["rmat"], 1)

                def p4_x2(n, u):
                    pv = W[0][:].rearrange("p (b m) -> p b m", b=2)[:, :, 0:DC * (CD + 1)].rearrange("p b (c k) -> p b c k", c=DC)
                    dve.wait_ge(s["pv1"], done(n, u))
                    nc.vector.reciprocal(rden1[:], pv[:, :, :, CD]).then_inc(s["rden1"], 1)
                    dve.wait_ge(s["rden1"], done(n, u))
                    for b in range(2):
                        ins = nc.vector.tensor_tensor(pvn[:, :, b, :], pv[:, b, :, 0:CD],
                                                      rden1[:, b, :].unsqueeze(2).broadcast_to([P, DC, CD]), ALU.mult)
                    ins.then_inc(s["pvn"], 1)
                    dve.wait_ge(s["pvn"], done(n, u))
                    dve.wait_ge(s["skip"], done(n, u))
                    if has(n, u, 2):
                        dve.wait_ge(s["ffn"], done(n, u, 2))
                    nc.vector.tensor_tensor(x2T[u][:].rearrange("p c t -> p (c t)"), M[3][:],
                                            pvn[:].rearrange("p c b k -> p (c b k)"), ALU.add).then_inc(s["x2T"], 1)

                def p5_stats(n, u):
                    dve.wait_ge(s["x2"], done(n, u))
                    nc.vector.bn_stats(st3[:], M[3][:]).then_inc(s["st3"], 1)
                    dve.wait_ge(s["st3"], done(n, u))
                    if has(n, u, 1):
                        dve.wait_ge(s["ve3"], done(n, u, 1))
                    dve.nop(nofuse=True)
                    nc.vector.bn_aggr(mv3[:], st3[:]).then_inc(s["mv3"], 1)

                def p5_y(n, u):
                    dve.wait_ge(s["ffn"], done(n, u))
                    dve.wait_ge(s["rs3"], done(n, u))
                    dve.wait_ge(s["x2b"], done(n, u))
                    if has(n, u, 2):
                        dve.wait_ge(y_out[u], nth(n - 1, 1))
                    nc.vector.scalar_tensor_tensor(y[u][:], M[3][:], rs3[:], x2b[:], ALU.mult, ALU.add).then_inc(s["y"], 1)

                if n[3] is not None:
                    p4_rmat(n[3], 1 - r)
                if n[0] is not None:
                    p1_norm(n[0], r)
                if n[1] is not None:
                    p2_max(n[1], 1 - r, 0)
                if n[0] is not None:
                    p1_xn(n[0], r)
                if n[1] is not None:
                    p2_max(n[1], 1 - r, 1)
                if n[4] is not None:
                    p5_stats(n[4], r)
                if n[2] is not None:
                    p3_ctx(n[2], r)
                if n[4] is not None:
                    p5_y(n[4], r)
                if n[3] is not None:
                    p4_max(n[3], 1 - r)
                if n[2] is not None:
                    p3_x1(n[2], r)
                if n[3] is not None:
                    p4_x2(n[3], 1 - r)

            run(dve, step)

        @block.tensor
        def _(pe):
            mm = nc.tensor.matmul
            tr = nc.tensor.transpose
            pe.wait_ge(s["prep_pool"], 4)
            pe.wait_ge(s["ld_attn"], 96)
            for c in range(DC):
                ins = tr(M[0][0:QL, c * P:(c + 1) * P], wqd[:, c], identf[:])
            ins.then_inc(s["wqdT_ps"], 1)
            pe.wait_ge(s["ld_vo"], 64)
            pe.wait_ge(s["ld_ffn"], 128)
            for c in range(DC):
                ins = tr(M[1][:, c * LAT:(c + 1) * LAT], wvu[:, c * P:(c + 1) * P], identf[0:LAT, 0:LAT])
            ins = tr(M[1][:, DC * LAT:DC * LAT + DC], bvr[:], identf[0:DC, 0:DC])
            ins.then_inc(s["wvuT_ps"], 1)
            pe.wait_ge(s["w13p"], 1)
            mm(M[1][:, 32:33], w13p[:], bq13[:], start=True, stop=True)
            mm(M[1][:, 33:34], spread[:], lw[:], start=True, stop=True).then_inc(s["cols_ps"], 1)
            pe.wait_ge(s["wqdT"], 1)
            for c in range(DC):
                ins = mm(M[0][:, c * P:(c + 1) * P], wqdT[:, c * P:(c + 1) * P], w13p[0:QL, :], start=True, stop=True)
            ins.then_inc(s["wqc_ps"], 1)
            pe.wait_ge(s["ld_x"], 112)
            mm(M[2][:, 0:CD], xwk[:].rearrange("p a b -> p (a b)"), xwq[:], start=True, stop=True)
            tr(M[2][:, 64:128], xwv[:].rearrange("p a b -> p (a b)"), identf[0:CD, 0:CD])
            tr(M[2][:, 128:192], xws[:].rearrange("p a b -> p (a b)"), identf[0:CD, 0:CD]).then_inc(s["xw_ps"], 1)
            for c in range(DC):
                ins = tr(W[0][:, c * P:(c + 1) * P], lb[:, c].rearrange("p n r -> p (n r)"), identf[:])
            ins.then_inc(s["lbT_ps"], 1)
            pe.wait_ge(s["vbd"], 1)
            for c in range(DC):
                ins = mm(M[3][:], vbd[:, c].rearrange("p h j -> p (h j)"), wo[:, c], start=(c == 0), stop=(c == DC - 1))
            ins.then_inc(s["mout_ps"], 1)
            for c in range(DC):
                ins = mm(W[0][:, 512:1024], bvT[:, c:c + 1].broadcast_to([P, P]), wo[:, c], start=(c == 0), stop=(c == DC - 1))
            ins.then_inc(s["cvec_ps"], 1)
            pe.wait_ge(s["cvec"], 1)
            for k in range(DC):
                for c in range(DC):
                    ins = tr(W[k // 2][:, (k % 2) * 512 + c * P:(k % 2) * 512 + (c + 1) * P], fw[:, c, k * P:(k + 1) * P], identf[:])
                ins.then_inc(s["wT_ps"], 1)
            pe.wait_ge(s["wqc"], 1)
            for k in range(DC):
                if k >= 2:
                    pe.wait_ge(s["weff"], k - 1)
                mm(M[k % 2][:], la[:, k * P:(k + 1) * P], lbT[:], start=True, stop=True).then_inc(s["lora_ps"], 1)
            pe.wait_ge(s["xw"], 1)
            pe.wait_ge(s["weff"], DC)
            for k in range(DC):
                ins = mm(M[2][:], meanw[:], weff[:, k], start=(k == 0), stop=(k == DC - 1))
            ins.then_inc(s["wmean_ps"], 1)
            pe.wait_ge(s["wcen"], DC)

            def step(r, n):
                def p1_xT(n, u):
                    pe.wait_ge(s["xn"], done(n, u))
                    if has(n, u, 1):
                        pe.wait_ge(s["cst"], done(n, u, 1))
                    for c in range(DC):
                        ins = tr(M[0][:, c * P:(c + 1) * P], xn[u][:, c * P:(c + 1) * P], identf[:])
                    ins.then_inc(s["xT"], 1)

                def p1_qc(n, u):
                    pe.wait_ge(s["xnT"], done(n, u))
                    for c in range(DC):
                        mm(M[0][:, 0:P], wqc[:, c], xnT[:, c], start=(c == 0), stop=(c == DC - 1))
                    for c in range(DC):
                        ins = mm(M[0][:, P:P + LAT], xnT[:, c], wkv[:, c], start=(c == 0), stop=(c == DC - 1))
                    ins.then_inc(s["qc"], 1)

                def p1_cT(n, u):
                    pe.wait_ge(s["ctile"], done(n, u))
                    pe.wait_ge(s["c32"], done(n, u))
                    tr(M[0][:].bitcast(BF16)[:, 0:P], ctile[u][:].rearrange("p b k -> p (b k)"), ident[:]).then_inc(s["cstT"], 1)

                def p2_scores(n, u, b):
                    if has(n, u, 3):
                        pe.wait_ge(s["pvn" if b == 0 else "e1"], done(n, u, 3))
                    elif has(n, u, 2):
                        pe.wait_ge(s[f"e0_{b}"], done(n, u, 2))
                    elif has(n, u, 1):
                        pe.wait_ge(s[f"mx0_{b}"], done(n, u, 1))
                    pe.wait_ge(q_in[u], nth(n, 6))
                    pe.wait_ge(s["cst"], done(n, u))
                    rows = slice(64 * b, 64 * b + KROWS)
                    for h in range(HP):
                        ins = mm(W[b][:, h * S:(h + 1) * S], qst[u][rows, h * P:(h + 1) * P], cst[u][rows, 64 * b:64 * b + 64],
                                 start=True, stop=True)
                    ins.then_inc(s[f"a0_{b}"], 1)

                def p2_maxT(n, u):
                    if has(n, u, 2):
                        pe.wait_ge(s["ctx_lo"], done(n, u, 2))
                    elif has(n, u, 1):
                        pe.wait_ge(s["mx0T"], done(n, u, 1))
                    pe.wait_ge(s["ml0"], done(n, u))
                    tr(M[1][:].bitcast(BF16)[0:2 * NPART * HP, 0:P], mp0[:].rearrange("p b a h -> p (b a h)"), ident[:])\
                        .then_inc(s["mT0"], 1)

                def p3_scores(n, u, k):
                    if not last(n, u):
                        pe.wait_ge(s[f"mx0_{k}"], done(n, u, -1))
                    else:
                        pe.wait_ge(s["pvn" if k == 0 else "e1"], done(n, u, 2))
                    pe.wait_ge(m_in[u], nth(n, 2))
                    for c in range(2):
                        col = k * WIDE + c * 512
                        ins = mm(W[k][:, c * 512:(c + 1) * 512], cst[u][0:64 + KALL, :], qst[u][0:64 + KALL, col:col + 512],
                                 start=True, stop=True)
                    ins.then_inc(s[f"b0_{k}"], 1)

                def p3_values(n, u):
                    if not last(n, u):
                        pe.wait_ge(s["mx0T"], done(n, u, -1))
                    elif has(n, u, 1):
                        pe.wait_ge(s["ctx_lo"], done(n, u, 1))
                    pe.wait_ge(s["cbd"], done(n, u))
                    for h in range(HP):
                        if h % (HP // 2) == 0:
                            pe.wait_ge(s[f"e0_{h // (HP // 2)}"], done(n, u))
                        ins = mm(M[1][:, h * 2 * (LAT + 1):(h + 1) * 2 * (LAT + 1)], p0[:, h * P:(h + 1) * P],
                                 cbd[u][:].rearrange("p b j -> p (b j)"), start=True, stop=True)
                    ins.then_inc(s["pv0"], 1)

                def p3_ctxT(n, u):
                    pe.wait_ge(s["ctxn"], done(n, u))
                    if has(n, u, 1):
                        pe.wait_ge(s["v"], done(n, u, 1))
                    pe.nop(nofuse=True)
                    for k in range(2):
                        rows = slice(64 * k, 64 * k + 64)
                        for b in range(2):
                            ins = mm(M[1 + k][rows, b * 64:b * 64 + 64], ctxn[rows, b].rearrange("p h j -> p (h j)"),
                                     identf[rows, 64 * k:64 * k + 64], start=True, stop=True)
                        ins.then_inc(s["ctxTa" if k == 0 else "ctxTb"], 1)

                def p3_out(n, u):
                    pe.wait_ge(s["ctx_lo"], done(n, u))
                    pe.wait_ge(s["ctx_hi"], done(n, u))
                    mm(M[2][:], ctxT[:], mout[:], start=True, stop=True).then_inc(s["o"], 1)

                def p4_gv(n, u):
                    pe.wait_ge(s["x1"], done(n, u))
                    pe.wait_ge(ld_c[u], nth(n, 1))
                    mm(M[2][:, 0:CM], kq[:], cin[u][:], start=True, stop=True)
                    mm(M[2][:, CM:CM + P], cin[u][:], wvbd[:], start=True, stop=True).then_inc(s["gv"], 1)

                def p4_a(n, u):
                    if not last(n, u):
                        pe.wait_ge(s["e0_0"], done(n, u, -1))
                    else:
                        pe.wait_ge(s["pvn"], done(n, u, 1))
                    pe.wait_ge(s["g"], done(n, u))
                    pe.wait_ge(s["x1c"], done(n, u))
                    for b in range(2):
                        rows = slice(64 * b, 64 * b + 64)
                        for c in range(DC):
                            col = b * 512 + c * P
                            ins = mm(W[0][:, col:col + P], x1c[u][rows, c * P:(c + 1) * P], g[rows, :], start=True, stop=True)
                    ins.then_inc(s["xa"], 1)

                def p4_b(n, u):
                    if not last(n, u):
                        pe.wait_ge(s["e0_1"], done(n, u, -1))
                    else:
                        pe.wait_ge(s["e1"], done(n, u, 1))
                    for b in range(2):
                        rows = slice(64 * b, 64 * b + 64)
                        mm(W[1][:, b * 512:(b + 1) * 512], g[rows, :], x1c[u][rows, :], start=True, stop=False, skip_group_check=True)
                    pe.wait_ge(s["ml1"], done(n, u))
                    for b in range(2):
                        for c in range(DC):
                            col = b * 512 + c * P
                            for k in range(NPART):
                                ins = mm(W[1][:, col:col + P], mp1[:, k, b, c:c + 1].broadcast_to([P, P]), negid[:],
                                         start=False, stop=(k == NPART - 1), skip_group_check=True)
                    ins.then_inc(s["xb"], 1)

                def p4_skip(n, u):
                    if has(n, u, 1):
                        pe.wait_ge(s["y"], done(n, u, 1))
                    pe.wait_ge(s["rmat"], done(n, u))
                    for c in range(DC):
                        ins = mm(M[3][:, c * P:(c + 1) * P], x1c[u][:, c * P:(c + 1) * P], rmat[:], start=True, stop=True)
                    ins.then_inc(s["skip"], 1)

                def p4_values(n, u):
                    pe.wait_ge(s["e1"], done(n, u))
                    pe.wait_ge(s["mx1"], done(n, u))
                    pe.wait_ge(s["v"], done(n, u))
                    for b in range(2):
                        for c in range(DC):
                            col = b * 512 + c * (CD + 1)
                            ins = mm(W[0][:, col:col + CD + 1], pt[:, b, c * P:(c + 1) * P], v65[u][:, b, :], start=True, stop=True)
                    ins.then_inc(s["pv1"], 1)

                def p5_x2(n, u):
                    pe.wait_ge(s["x2T"], done(n, u))
                    for c in range(DC):
                        ins = tr(M[3][:, c * P:(c + 1) * P], x2T[u][:, c, :], identf[:])
                    ins.then_inc(s["x2"], 1)

                def p5_ffn(n, u):
                    pe.wait_ge(s["x2s"], done(n, u))
                    for c in range(DC):
                        ins = mm(M[3][:], x2T[u][:, c, :], weff[:, c], start=(c == 0), stop=(c == DC - 1))
                    ins.then_inc(s["ffn"], 1)

                if n[3] is not None:
                    p4_gv(n[3], 1 - r)
                if n[1] is not None:
                    p2_scores(n[1], 1 - r, 0)
                    p2_scores(n[1], 1 - r, 1)
                if n[4] is not None:
                    p5_x2(n[4], r)
                if n[0] is not None:
                    p1_xT(n[0], r)
                if n[2] is not None:
                    p3_scores(n[2], r, 0)
                if n[0] is not None:
                    p1_qc(n[0], r)
                if n[2] is not None:
                    p3_scores(n[2], r, 1)
                if n[4] is not None:
                    p5_ffn(n[4], r)
                if n[1] is not None:
                    p2_maxT(n[1], 1 - r)
                if n[2] is not None:
                    p3_values(n[2], r)
                if n[3] is not None:
                    p4_a(n[3], 1 - r)
                if n[0] is not None:
                    p1_cT(n[0], r)
                if n[2] is not None:
                    p3_ctxT(n[2], r)
                if n[3] is not None:
                    p4_b(n[3], 1 - r)
                if n[2] is not None:
                    p3_out(n[2], r)
                if n[3] is not None:
                    p4_skip(n[3], 1 - r)
                    p4_values(n[3], 1 - r)

            run(pe, step)


_INS = ["x", "ctx_1024", "L0_attn_Wq_d", "L0_attn_bq_d", "L0_attn_W_qk", "L0_attn_b_qk", "L0_attn_Wkv_d",
        "L0_attn_bkv_d", "L0_attn_Wv_u", "L0_attn_bv_u", "L0_attn_Wo", "L0_attn_bo", "L0_xattn_Wq", "L0_xattn_Wk",
        "L0_xattn_Wv", "L0_xattn_Wskip", "L0_ffn_lora_A", "L0_ffn_lora_B", "L0_ffn_W", "L0_ffn_bias",
        "L0_ffn_lora_weights"]


def kernel(**inputs):
    import numpy as _np
    import concourse.bacc as _bacc
    from concourse import mybir as _mybir
    from concourse.bass_utils import run_bass_kernel_spmd as _run

    nc = _bacc.Bacc("TRN2", target_bir_lowering=False, num_devices=1)
    arrays, io = {}, {}
    for name in _INS:
        a = _np.ascontiguousarray(inputs[name])
        arrays[f"in_{name}"] = a
        io[name] = nc.dram_tensor(f"in_{name}", a.shape, _mybir.dt.from_np(a.dtype), kind="ExternalInput").ap()
    io["out"] = nc.dram_tensor("out_y", inputs["x"].shape, _mybir.dt.float32, kind="ExternalOutput").ap()
    decoder(nc, io)
    r = _run(nc, [arrays], core_ids=[0])
    return r.results[0]["out_y"]
```

```python
from contextlib import ExitStack

import concourse.bass as bass
from concourse import mybir

F32 = mybir.dt.float32
BF16 = mybir.dt.bfloat16
F16 = mybir.dt.float16
ALU = mybir.AluOpType
ACT = mybir.ActivationFunctionType
AX_X = mybir.AxisListType.X

P = 128
B, S, D = 32, 64, 512
PAIRS = B * S // P
DC = D // P
H, LAT, QL = 32, 4, 12
HP = H // 2
HD = D // H
CD, CM = S, P
NL, RANK, ALPHA = 8, 16, 32
EPS = 1e-5
NPART = 3
KROWS = NPART * NPART * LAT
KALL = KROWS + NPART
MROWS = DC * 2 * NPART
LN_TOP = 15 * 0.6931471805599453
WIDE = 2 * 512


def done(n, u, back=0):
    return 2 * n + (u + 1 - back)


def decoder(nc, io):
    x_d = io["x"].rearrange("b s d -> (b s) d")
    ctx_d = io["ctx_1024"].rearrange("b c m -> (b c) m")
    out_d = io["out"].rearrange("b s d -> (b s) d")
    es = ExitStack()
    with es:
        def sb(name, shape, dt=F32):
            return es.enter_context(nc.sbuf_tensor(name, shape, dt))

        def sem(name):
            return es.enter_context(nc.semaphore(name))

        cmask = sb("cmask", [MROWS, DC, P])
        bsel4 = sb("bsel4", [MROWS, DC, 2])
        nsel = sb("nsel", [MROWS, 2])
        nselb = sb("nselb", [MROWS, 2], BF16)
        identf = sb("identf", [P, P])
        ident = sb("ident", [P, P], BF16)
        half36 = sb("half36", [P, 2, KROWS], BF16)
        half5 = sb("half5", [P, NPART, 2, LAT], BF16)
        mhalf = sb("mhalf", [P, 1])
        epsc = sb("epsc", [P, 1])
        ones = sb("ones", [P, P])
        meanw = sb("meanw", [P, P])
        wqd = sb("wqd", [P, DC, QL])
        w13 = sb("w13", [QL + 1, P])
        w13p = sb("w13p", [QL + 1, P])
        bq13 = sb("bq13", [QL + 1, 1])
        wqdT = sb("wqdT", [QL, D])
        wqc = sb("wqc", [P, DC, P + LAT])
        bqc = sb("bqc", [P, P + LAT])
        wvu = sb("wvu", [LAT, D])
        vT = sb("vT", [P, DC * LAT + DC])
        wvuT = vT[:, 0:DC * LAT].rearrange("p (c j) -> p c j", j=LAT)
        hmask = sb("hmask", [P, DC, H])
        vbd = sb("vbd", [P, DC, H, LAT])
        wo = sb("wo", [P, DC, D])
        bvr = sb("bvr", [DC, P])
        bvT = vT[:, DC * LAT:DC * LAT + DC]
        bo = sb("bo", [P, D])
        mout = sb("mout", [P, D])
        cvec = sb("cvec", [P, D])
        xwk = sb("xwk", [CD, 2, CD])
        xwq = sb("xwq", [CD, CD])
        xwv = sb("xwv", [CD, 2, CD])
        xws = sb("xws", [CD, 2, CD])
        kq = sb("kq", [P, P])
        wvbd = sb("wvbd", [P, P])
        wsbd = sb("wsbd", [P, P])
        fw = sb("fw", [P, DC, D])
        la = sb("la", [P, D])
        lb = sb("lb", [P, DC, NL, RANK])
        lbT = sb("lbT", [P, D])
        lw = sb("lw", [NL, 1])
        spread = sb("spread", [NL, P])
        coef = sb("coef", [P, 1])
        weff = sb("weff", [P, DC, D])
        fbias = sb("fbias", [P, D])

        def two(name, shape, dt=F32):
            return [sb(f"{name}{u}", shape, dt) for u in range(2)]

        xin = two("xin", [P, D])
        st1 = sb("st1", [P, 6])
        mv1 = sb("mv1", [P, 2])
        rs1 = sb("rs1", [P, 2])
        xn = two("xn", [P, D])
        x0b = two("x0b", [P, D])
        xnT = sb("xnT", [P, DC, P])
        qc = sb("qc", [P, P + LAT])
        qr = sb("qr", [P, P + LAT])
        qcp = sb("qcp", [P, NPART, P + LAT], BF16)
        qpart = two("qpart", [P, 2, NPART, S], BF16)
        ctile = two("ctile", [P, 2, S], BF16)
        cbd = two("cbd", [P, NPART, 2, LAT + 1], BF16)
        cst = two("cst", [P, P], BF16)
        qst = two("qst", [P, H * S], BF16)
        mx0 = two("mx0", [P, 2, HP])
        mr0 = sb("mr0", [P, 2, HP])
        mp0 = sb("mp0", [P, 2, NPART, HP], BF16)
        mx0T = two("mx0T", [2 * NPART * HP, P], BF16)
        p0 = sb("p0", [P, H * S])
        p0h = sb("p0h", [P, H * S], F16)
        p0l = sb("p0l", [P, H * S], F16)
        pv5 = sb("pv5", [P, HP, 2, LAT + 1])
        lntop = sb("lntop", [P, 1])
        rden0 = sb("rden0", [P, 2, HP])
        ctxn = sb("ctxn", [P, 2, HP, LAT])
        ctxT = sb("ctxT", [P, P])
        x1 = sb("x1", [P, D])
        st2 = sb("st2", [P, 6])
        mv2 = two("mv2", [P, 2])
        ve2 = sb("ve2", [P, 1])
        rs2 = two("rs2", [P, 1])
        x1c = two("x1c", [P, D])
        cin = two("cin", [P, CM])
        g = sb("g", [P, CM])
        v65 = two("v65", [P, 2, CD + 1])
        mx1 = sb("mx1", [P, 2, DC])
        mr1 = sb("mr1", [P, DC, 2])
        mp1 = sb("mp1", [P, DC, 2, NPART], BF16)
        mexp = sb("mexp", [MROWS, DC, P], BF16)
        pt = sb("pt", [P, 2, D])
        rmat = sb("rmat", [P, P])
        rden1 = sb("rden1", [P, 2, DC])
        pvn = sb("pvn", [P, DC, 2, CD])
        x2T = two("x2T", [P, DC, P])
        st3 = sb("st3", [P, 6])
        mv3 = sb("mv3", [P, 2])
        ve3 = sb("ve3", [P, 1])
        rs3 = sb("rs3", [P, 1])
        x2s = sb("x2s", [P, D])
        x2b = sb("x2b", [P, D])
        y = two("y", [P, D])

        q_scr = [nc.dram_tensor(f"q_scr{u}", (2 * NPART, P, S), BF16, kind="Internal").ap() for u in range(2)]
        m_scr = [nc.dram_tensor(f"m_scr{u}", (2 * NPART * HP, P), BF16, kind="Internal").ap() for u in range(2)]

        W = [es.enter_context(nc.psum_tensor(f"wide{k}", [P, WIDE], F32)) for k in range(2)]
        M = [es.enter_context(nc.psum_tensor(f"bank{k}", [P, 512], F32)) for k in range(4)]

        names = """ld_attn ld_vo ld_x ld_ffn prep_pool wqdT_ps wvuT_ps cols_ps wqc_ps xw_ps lbT_ps mout_ps w13p halves bsel4 nsel nselb cvec_ps wT_ps lora_ps wmean_ps wqdT wvuT coef wqc xw mout wT vbd lbT cvec weff wcen
        st1 mv1 ve1 rs1 xn xT xnT x0b qc_ps qc qh qr qm ql cbd ctile qT qpart cstT cst
        a0_0 a0_1 mx0_0 mx0_1 mh0 mr0 mm0 ml0 mT0 mx0T b0_0 b0_1 e0_0 e0_1 p0h_0 p0h_1 p0l_0 p0l_1 pv5 pv0 rden0 ctxn ctxTa ctxTb ctx_lo ctx_hi
        o x1 st2 mv2 ve2 rs2 x1c gv g v xa mx1 mh1 mr1 mm1 ml1 mT1 mexp xb e1 rmat skip pv1 rden1 pvn x2T
        x2 st3 mv3 ve3 rs3 x2s ffn x2b y"""
        s = {n: sem("s_" + n) for n in names.split()}
        ld_x = [sem(f"s_xin{u}") for u in range(2)]
        ld_c = [sem(f"s_cin{u}") for u in range(2)]
        q_out = [sem(f"s_qout{u}") for u in range(2)]
        q_in = [sem(f"s_qin{u}") for u in range(2)]
        m_out = [sem(f"s_mout{u}") for u in range(2)]
        m_in = [sem(f"s_min{u}") for u in range(2)]
        y_out = [sem(f"s_stored{u}") for u in range(2)]

        PHASES = 6
        FIRST = PHASES + 2

        def run(eng, step):
            def pairs(i):
                return [(i - k) // 2 if 0 <= i - k < PAIRS else None for k in range(PHASES)]
            for i in range(FIRST):
                step(i % 2, pairs(i))
            with eng.Fori(FIRST // 2, PAIRS // 2) as j:
                for r in range(2):
                    step(r, [j + (r - k) // 2 if (r - k) // 2 else j for k in range(PHASES)])
            for i in range(PAIRS, PAIRS + PHASES - 1):
                step(i % 2, pairs(i))

        def has(n, u, back):
            return not isinstance(n, int) or 2 * n + u >= back

        def last(n, u, ahead=1):
            return isinstance(n, int) and 2 * n + u + ahead >= PAIRS

        def nth(n, k):
            return n * (16 * k) + 16 * k

        block = es.enter_context(nc.Block())

        @block.sync
        def _(sp):
            sp.dma_start(wqd[:], io["L0_attn_Wq_d"].rearrange("(c p) k -> p c k", p=P)).then_inc(s["ld_attn"], 16)
            sp.dma_start(w13[0:QL, :], io["L0_attn_W_qk"]).then_inc(s["ld_attn"], 16)
            sp.dma_start(w13[QL:QL + 1, :], io["L0_attn_b_qk"].rearrange("(a n) -> a n", a=1)).then_inc(s["ld_attn"], 16)
            sp.wait_ge(s["prep_pool"], 1)
            sp.dma_start(bq13[0:QL, :], io["L0_attn_bq_d"].rearrange("(n a) -> n a", a=1)).then_inc(s["ld_attn"], 16)
            sp.dma_start(wqc[:, :, P:P + LAT], io["L0_attn_Wkv_d"].rearrange("(c p) k -> p c k", p=P)).then_inc(s["ld_attn"], 16)
            sp.dma_start(bqc[:, P:P + LAT], io["L0_attn_bkv_d"].rearrange("(a n) -> a n", a=1).broadcast_to([P, LAT])).then_inc(s["ld_attn"], 16)

            def step(r, n):
                def p2_out(n, u):
                    sp.wait_ge(s["mx0T"], done(n, u))
                    sp.nop(nofuse=True)
                    sp.dma_start(m_scr[u], mx0T[u][:]).then_inc(m_out[u], 16)

                def p2_in(n, u):
                    sp.wait_ge(m_out[u], nth(n, 1))
                    sp.nop(nofuse=True)
                    for b in range(2):
                        sp.dma_start(qst[u][64 * b + KROWS:64 * b + KALL, :],
                                     m_scr[u].rearrange("(b a h) q -> b a (h q)", b=2, a=NPART)[b]).then_inc(m_in[u], 16)

                def p1_out(n, u):
                    if has(n, u, 2):
                        sp.wait_ge(q_in[u], nth(n - 1, 6))
                        sp.nop(nofuse=True)
                    sp.wait_ge(s["qpart"], done(n, u))
                    sp.nop(nofuse=True)
                    sp.dma_start(q_scr[u].rearrange("k p q -> p k q"),
                                 qpart[u][:].rearrange("p b a q -> p (b a) q")).then_inc(q_out[u], 16)

                def p1_in(n, u):
                    sp.wait_ge(q_out[u], nth(n, 1))
                    sp.nop(nofuse=True)
                    if has(n, u, 2):
                        sp.wait_ge(s["b0_1"], done(n, u, 2))
                        sp.nop(nofuse=True)
                    for b in range(2):
                        rows = q_scr[u][NPART * b:NPART * (b + 1)].rearrange("a (j h) q -> (a j) (h q)", j=LAT)
                        for part in range(NPART):
                            r0 = 64 * b + part * NPART * LAT
                            sp.dma_start(qst[u][r0:r0 + NPART * LAT, :], rows).then_inc(q_in[u], 16)

                def p5_store(n, u):
                    sp.wait_ge(s["y"], done(n, u))
                    sp.nop(nofuse=True)
                    sp.dma_start(out_d[bass.ds((n * 2 + u) * P, P), :], y[u][:]).then_inc(y_out[u], 16)

                if n[2] is not None:
                    p2_out(n[2], r)
                if n[1] is not None:
                    p1_out(n[1], 1 - r)
                if n[1] is not None:
                    p1_in(n[1], 1 - r)
                if n[2] is not None:
                    p2_in(n[2], r)
                if n[5] is not None:
                    p5_store(n[5], 1 - r)

            run(sp, step)
            for u in range(2):
                sp.wait_ge(y_out[u], nth(PAIRS // 2 - 1, 1))

        @block.gpsimd
        def _(pool):
            nc.gpsimd.memset(bq13[:], 1.0).then_inc(s["prep_pool"], 1)
            nc.gpsimd.memset(identf[:], 0.0)
            nc.gpsimd.memset(mhalf[:], -0.5)
            nc.gpsimd.memset(epsc[:], EPS)
            nc.gpsimd.memset(lntop[:], LN_TOP)
            nc.gpsimd.memset(ones[:], 1.0)
            nc.gpsimd.memset(meanw[:], 1.0 / D)
            for t_ in (half36, half5, kq, wvbd, wsbd):
                nc.gpsimd.memset(t_[:], 0.0)
            nc.gpsimd.memset(spread[:], 1.0)
            for u in range(2):
                nc.gpsimd.memset(ctile[u][:], 0.0)
                nc.gpsimd.memset(qst[u][:], 0.0)
                nc.gpsimd.memset(v65[u][:], 1.0)
                nc.gpsimd.memset(cbd[u][:], 0.0)
            nc.gpsimd.memset(cmask[:], 1.0)
            nc.gpsimd.memset(bsel4[:], 1.0)
            nc.gpsimd.memset(hmask[:], 1.0).then_inc(s["prep_pool"], 1)
            pool.wait_ge(s["prep_pool"], 2)
            nc.gpsimd.affine_select(out=hmask[:], in_=hmask[:], compare_op=ALU.is_ge, fill=0.0, base=0,
                                    pattern=[[P, DC], [-HD, 2], [-2 * HD, HP]], channel_multiplier=1)
            nc.gpsimd.affine_select(out=cmask[:], in_=cmask[:], compare_op=ALU.is_ge, fill=0.0, base=0,
                                    pattern=[[-2 * NPART, DC], [0, P]], channel_multiplier=1)
            nc.gpsimd.affine_select(out=bsel4[:], in_=bsel4[:], compare_op=ALU.is_ge, fill=0.0, base=0,
                                    pattern=[[-2 * NPART, DC], [-NPART, 2]], channel_multiplier=1)
            nc.gpsimd.affine_select(out=spread[:], in_=spread[:], compare_op=ALU.is_ge, fill=0.0, base=0,
                                    pattern=[[1, P]], channel_multiplier=-RANK)
            nc.gpsimd.affine_select(out=identf[:], in_=identf[:], compare_op=ALU.not_equal, fill=1.0, base=0,
                                    pattern=[[-1, P]], channel_multiplier=1).then_inc(s["prep_pool"], 1)
            pool.wait_ge(s["prep_pool"], 3)
            nc.gpsimd.affine_select(out=hmask[:], in_=hmask[:], compare_op=ALU.is_ge, fill=0.0, base=HD - 1,
                                    pattern=[[-P, DC], [HD, 2], [2 * HD, HP]], channel_multiplier=-1)
            nc.gpsimd.affine_select(out=cmask[:], in_=cmask[:], compare_op=ALU.is_ge, fill=0.0, base=2 * NPART - 1,
                                    pattern=[[2 * NPART, DC], [0, P]], channel_multiplier=-1)
            nc.gpsimd.affine_select(out=bsel4[:], in_=bsel4[:], compare_op=ALU.is_ge, fill=0.0, base=NPART - 1,
                                    pattern=[[2 * NPART, DC], [NPART, 2]], channel_multiplier=-1).then_inc(s["bsel4"], 1)
            nc.gpsimd.affine_select(out=spread[:], in_=spread[:], compare_op=ALU.is_ge, fill=0.0, base=RANK - 1,
                                    pattern=[[-1, P]], channel_multiplier=RANK)
            nc.gpsimd.tensor_copy(ident[:], identf[:]).then_inc(s["prep_pool"], 1)

            pool.wait_ge(s["ld_attn"], 96)
            nc.gpsimd.tensor_copy(w13p[:].rearrange("c (j h) -> c j h", j=LAT),
                                  w13[:].rearrange("c (h j) -> c j h", j=LAT)).then_inc(s["w13p"], 1)

            def rstd(ve, var, out, wait_var, ve_done, rs_done, n, u):
                pool.wait_ge(s[wait_var], done(n, u))
                nc.gpsimd.tensor_tensor(ve, var, epsc[:], ALU.add).then_inc(s[ve_done], 1)
                pool.wait_ge(s[ve_done], done(n, u))
                nc.gpsimd.tensor_tensor(out, ve, mhalf[:], ALU.pow).then_inc(s[rs_done], 1)

            def step(r, n):
                def p1_rstd(n, u):
                    rstd(rs1[:, 1:2], mv1[:, 1:2], rs1[:, 0:1], "mv1", "ve1", "rs1", n, u)

                def p1_residual(n, u):
                    if not has(n, u, 1):
                        pool.wait_ge(s["cvec"], 1)
                    if has(n, u, 2):
                        pool.wait_ge(s["x1"], done(n, u, 2))
                    pool.wait_ge(ld_x[u], nth(n, 1))
                    nc.gpsimd.tensor_tensor(x0b[u][:], xin[u][:], cvec[:], ALU.add).then_inc(s["x0b"], 1)

                def p1_q(n, u):
                    one = ones[:, 0:1].broadcast_to([P, P + LAT])
                    pool.wait_ge(s["qh"], done(n, u))
                    if has(n, u, 1):
                        pool.wait_ge(s["qT"], done(n, u, 1))
                    nc.gpsimd.tensor_tensor(qr[:], qc[:], qcp[:, 0, :], ALU.subtract).then_inc(s["qr"], 1)
                    pool.wait_ge(s["qr"], done(n, u))
                    nc.gpsimd.tensor_tensor(qcp[:, 1, :], qr[:], one, ALU.mult).then_inc(s["qm"], 1)
                    pool.wait_ge(s["qm"], done(n, u))
                    nc.gpsimd.tensor_tensor(qcp[:, 2, :], qr[:], qcp[:, 1, :], ALU.subtract).then_inc(s["ql"], 1)
                    if has(n, u, 2):
                        pool.wait_ge(s["cstT"], done(n, u, 2))
                    pool.wait_ge(s["ql"], done(n, u))
                    for b in range(2):
                        ins = nc.gpsimd.tensor_tensor(
                            ctile[u][:, b, 0:KROWS].rearrange("p (k a j) -> p k a j", k=NPART, a=NPART),
                            qcp[:, :, P:P + LAT].unsqueeze(2).broadcast_to([P, NPART, NPART, LAT]),
                            half36[:, b, :].rearrange("p (k a j) -> p k a j", k=NPART, a=NPART), ALU.mult)
                    ins.then_inc(s["ctile"], 1)

                def p1_values(n, u):
                    if has(n, u, 2):
                        pool.wait_ge(s["pv0"], done(n, u, 2))
                    for b in range(2):
                        ins = nc.gpsimd.tensor_tensor(cbd[u][:, :, b, 0:LAT], qcp[:, :, P:P + LAT], half5[:, :, b, :], ALU.mult)
                    ins.then_inc(s["cbd"], 1)

                def split(x, one, parts, rest, sx, h, mid, rr, low, n, u):
                    for k in sx:
                        pool.wait_ge(s[k], done(n, u))
                    nc.gpsimd.tensor_tensor(parts[0], x, one, ALU.mult).then_inc(s[h], 1)
                    pool.wait_ge(s[h], done(n, u))
                    nc.gpsimd.tensor_tensor(rest, x, parts[0], ALU.subtract).then_inc(s[rr], 1)
                    pool.wait_ge(s[rr], done(n, u))
                    nc.gpsimd.tensor_tensor(parts[1], rest, one, ALU.mult).then_inc(s[mid], 1)
                    pool.wait_ge(s[mid], done(n, u))
                    nc.gpsimd.tensor_tensor(parts[2], rest, parts[1], ALU.subtract).then_inc(s[low], 1)

                def p2_split(n, u):
                    if has(n, u, 1):
                        pool.wait_ge(s["mT0"], done(n, u, 1))
                    split(mx0[u][:], ones[:, 0:2 * HP].rearrange("p (b h) -> p b h", b=2), [mp0[:, :, k, :] for k in range(NPART)], mr0[:],
                          ("mx0_0", "mx0_1"), "mh0", "mm0", "mr0", "ml0", n, u)

                def p3_rstd(n, u):
                    if has(n, u, 2):
                        pool.wait_ge(s["rmat"], done(n, u, 2))
                        pool.wait_ge(s["g"], done(n, u, 2))
                    rstd(ve2[:], mv2[u][:, 1:2], rs2[u][:], "mv2", "ve2", "rs2", n, u)

                def p4_split(n, u):
                    if has(n, u, 1):
                        pool.wait_ge(s["mT1"], done(n, u, 1))
                    split(mx1[:].rearrange("p b c -> p c b"), ones[:, 0:2 * DC].rearrange("p (c b) -> p c b", b=2),
                          [mp1[:, :, :, k] for k in range(NPART)], mr1[:], ("mx1",), "mh1", "mm1", "mr1", "ml1", n, u)

                def p5_rstd(n, u):
                    if has(n, u, 1):
                        pool.wait_ge(s["y"], done(n, u, 1))
                    rstd(ve3[:], mv3[:, 1:2], rs3[:], "mv3", "ve3", "rs3", n, u)

                def p5_bias(n, u):
                    pool.wait_ge(s["x2s"], done(n, u))
                    if has(n, u, 1):
                        pool.wait_ge(s["y"], done(n, u, 1))
                    nc.gpsimd.tensor_tensor(x2b[:], x2s[:], fbias[:], ALU.add).then_inc(s["x2b"], 1)

                if n[2] is not None:
                    p1_residual(n[2], r)
                if n[2] is not None:
                    p2_split(n[2], r)
                if n[1] is not None:
                    p1_q(n[1], 1 - r)
                if n[0] is not None:
                    p1_rstd(n[0], r)
                if n[4] is not None:
                    p4_split(n[4], r)
                if n[5] is not None:
                    p5_rstd(n[5], 1 - r)
                if n[5] is not None:
                    p5_bias(n[5], 1 - r)
                if n[1] is not None:
                    p1_values(n[1], 1 - r)
                if n[3] is not None:
                    p3_rstd(n[3], 1 - r)

            pool.wait_ge(s["halves"], 1)
            pool.wait_ge(s["ld_ffn"], 16 * 8)
            run(pool, step)

        @block.scalar
        def _(act):
            act.dma_start(wvu[:], io["L0_attn_Wv_u"]).then_inc(s["ld_vo"], 16)
            act.dma_start(wo[:], io["L0_attn_Wo"].rearrange("(c p) n -> p c n", p=P)).then_inc(s["ld_vo"], 16)
            act.dma_start(bvr[:], io["L0_attn_bv_u"].rearrange("(c p) -> c p", p=P)).then_inc(s["ld_vo"], 16)
            act.dma_start(bo[:], io["L0_attn_bo"].rearrange("(a n) -> a n", a=1).broadcast_to([P, D])).then_inc(s["ld_vo"], 16)
            act.dma_start(xwq[:], io["L0_xattn_Wq"]).then_inc(s["ld_x"], 16)
            for k in range(2):
                act.dma_start(xwk[:, k, :], io["L0_xattn_Wk"]).then_inc(s["ld_x"], 16)
                act.dma_start(xwv[:, k, :], io["L0_xattn_Wv"]).then_inc(s["ld_x"], 16)
                act.dma_start(xws[:, k, :], io["L0_xattn_Wskip"]).then_inc(s["ld_x"], 16)
            act.dma_start(fw[:], io["L0_ffn_W"].rearrange("(c p) n -> p c n", p=P)).then_inc(s["ld_ffn"], 16)
            act.dma_start(la[:], io["L0_ffn_lora_A"].rearrange("n r d -> (n r) d")).then_inc(s["ld_ffn"], 16)
            for c in range(DC):
                act.dma_start(lb[:, c], io["L0_ffn_lora_B"][:, c * P:(c + 1) * P, :].rearrange("n p r -> p n r")).then_inc(s["ld_ffn"], 16)
            act.dma_start(lw[:], io["L0_ffn_lora_weights"].rearrange("(n a) -> n a", a=1)).then_inc(s["ld_ffn"], 16)
            act.dma_start(fbias[:], io["L0_ffn_bias"].rearrange("(a n) -> a n", a=1).broadcast_to([P, D])).then_inc(s["ld_ffn"], 16)

            act.wait_ge(s["wqdT_ps"], 1)
            nc.scalar.copy(wqdT[:], M[0][0:QL, :]).then_inc(s["wqdT"], 1)
            act.wait_ge(s["cols_ps"], 1)
            nc.scalar.copy(vT[:], M[1][:, 0:DC * LAT + DC]).then_inc(s["wvuT"], 1)
            nc.scalar.copy(bqc[:, 0:P], M[1][:, 128:128 + P])
            nc.scalar.mul(coef[:], M[1][:, 33:34], float(ALPHA) / RANK).then_inc(s["coef"], 1)
            act.wait_ge(s["wqc_ps"], 1)
            nc.scalar.copy(wqc[:, :, 0:P], M[0][:].rearrange("p (c n) -> p c n", c=DC)).then_inc(s["wqc"], 1)
            act.wait_ge(s["xw_ps"], 1)
            for b in range(2):
                q_ = slice(64 * b, 64 * b + 64)
                nc.scalar.copy(kq[q_, q_], M[2][q_, 0:64])
                nc.scalar.copy(wvbd[q_, q_], M[2][q_, 64:128])
                fin = nc.scalar.copy(wsbd[q_, q_], M[2][q_, 128:192])
            fin.then_inc(s["xw"], 1)
            act.wait_ge(s["mout_ps"], 1)
            nc.scalar.copy(mout[:], M[3][:]).then_inc(s["mout"], 1)
            for k in range(DC):
                act.wait_ge(s["wT_ps"], k + 1)
                nc.scalar.copy(weff[:, k], W[k // 2][:, (k % 2) * 512:(k % 2) * 512 + 512]).then_inc(s["wT"], 1)

            def step(r, n):
                def p1_load(n, u):
                    if has(n, u, 2):
                        act.wait_ge(s["xn"], done(n, u, 2))
                        act.nop(nofuse=True)
                        act.wait_ge(s["x0b"], done(n, u, 2))
                        act.nop(nofuse=True)
                    act.dma_start(xin[u][:], x_d[bass.ds((n * 2 + u) * P, P), :]).then_inc(ld_x[u], 16)

                def p4_load(n, u):
                    if has(n, u, 2):
                        act.wait_ge(s["gv"], done(n, u, 2))
                        act.nop(nofuse=True)
                    act.dma_start(cin[u][:], ctx_d[bass.ds((n * 2 + u) * P, P), :]).then_inc(ld_c[u], 16)

                def p0_xT(n, u):
                    act.wait_ge(s["xT"], done(n, u))
                    if has(n, u, 1):
                        act.wait_ge(s["qc_ps"], done(n, u, 1))
                    nc.scalar.copy(xnT[:].rearrange("p c t -> p (c t)"), M[0][:]).then_inc(s["xnT"], 1)

                def p1_q(n, u):
                    act.wait_ge(s["qc"], done(n, u))
                    if has(n, u, 1):
                        act.wait_ge(s["qT"], done(n, u, 1))
                        act.wait_ge(s["cbd"], done(n, u, 1))
                    nc.scalar.copy(qcp[:, 0, :], qc[:]).then_inc(s["qh"], 1)

                def p1_qT(n, u):
                    act.wait_ge(s["cstT"], done(n, u))
                    if has(n, u, 2):
                        act.wait_ge(q_out[u], nth(n - 1, 1))
                    nc.scalar.copy(qpart[u][:].rearrange("p b a q -> p a b q"),
                                   M[0][:].bitcast(BF16)[:, P:P + NPART * P].rearrange("p (a b q) -> p a b q", a=NPART, b=2))\
                        .then_inc(s["qpart"], 1)

                def p1_c(n, u):
                    act.wait_ge(s["cstT"], done(n, u))
                    if has(n, u, 2):
                        act.wait_ge(s["b0_1"], done(n, u, 2))
                    nc.scalar.copy(cst[u][:], M[0][:].bitcast(BF16)[:, 0:P]).then_inc(s["cst"], 1)

                def p2_max(n, u):
                    act.wait_ge(s["mT0"], done(n, u))
                    if has(n, u, 2):
                        act.wait_ge(m_out[u], nth(n - 1, 1))
                    nc.scalar.copy(mx0T[u][:], M[1][:].bitcast(BF16)[0:2 * NPART * HP, 0:P]).then_inc(s["mx0T"], 1)

                def p3_exp(n, u, k):
                    act.wait_ge(s[f"b0_{k}"], done(n, u))
                    if has(n, u, 1):
                        act.wait_ge(s["pv0"], done(n, u, 1))
                    cols = slice(k * WIDE, (k + 1) * WIDE)
                    nc.scalar.activation(p0[:, cols], W[k][:], ACT.Exp, bias=lntop[:],
                                         scale=float(LAT) ** -0.5).then_inc(s[f"e0_{k}"], 1)

                def p3_high(n, u, k):
                    cols = slice(k * WIDE, (k + 1) * WIDE)
                    act.wait_ge(s[f"e0_{k}"], done(n, u))
                    nc.scalar.copy(p0h[:, cols], p0[:, cols]).then_inc(s[f"p0h_{k}"], 1)

                def p3_ctx(n, u):
                    act.wait_ge(s["ctxTb"], done(n, u))
                    if has(n, u, 1):
                        act.wait_ge(s["o"], done(n, u, 1))
                    nc.scalar.copy(ctxT[0:64, :], M[1][0:64, 0:P]).then_inc(s["ctx_lo"], 1)
                    nc.scalar.copy(ctxT[64:128, :], M[2][64:128, 0:P]).then_inc(s["ctx_hi"], 1)

                def p4_gv(n, u):
                    act.wait_ge(s["gv"], done(n, u))
                    act.wait_ge(s["rs2"], done(n, u))
                    if has(n, u, 1):
                        act.wait_ge(s["xb"], done(n, u, 1))
                    nc.scalar.activation(g[:], M[2][:, 0:CM], ACT.Copy, scale=rs2[u][:]).then_inc(s["g"], 1)
                    if has(n, u, 2):
                        act.wait_ge(s["pv1"], done(n, u, 2))
                    nc.scalar.copy(v65[u][:, :, 0:CD], M[2][:, CM:CM + P].rearrange("p (b c) -> p b c", b=2)).then_inc(s["v"], 1)

                def p4_exp(n, u):
                    act.wait_ge(s["xb"], done(n, u))
                    if has(n, u, 1):
                        act.wait_ge(s["pv1"], done(n, u, 1))
                    nc.scalar.activation(pt[:].rearrange("p b n -> p (b n)"), W[1][:], ACT.Exp,
                                         scale=float(CD) ** -0.5).then_inc(s["e1"], 1)

                def p5_x2(n, u):
                    act.wait_ge(s["x2"], done(n, u))
                    if has(n, u, 1):
                        act.wait_ge(s["st3"], done(n, u, 1))
                        act.wait_ge(s["x2b"], done(n, u, 1))
                    nc.scalar.activation(x2s[:], M[3][:], ACT.Identity, bias=mv2[u][:, 0:1]).then_inc(s["x2s"], 1)

                if n[4] is not None:
                    p4_gv(n[4], r)
                if n[0] is not None:
                    p1_load(n[0], r)
                if n[3] is not None:
                    p4_load(n[3], 1 - r)
                if n[5] is not None:
                    p5_x2(n[5], 1 - r)
                if n[3] is not None:
                    p3_exp(n[3], 1 - r, 0)
                if n[1] is not None:
                    p1_q(n[1], 1 - r)
                if n[3] is not None:
                    p3_exp(n[3], 1 - r, 1)
                if n[3] is not None:
                    p3_high(n[3], 1 - r, 0)
                if n[3] is not None:
                    p3_high(n[3], 1 - r, 1)
                if n[2] is not None:
                    p2_max(n[2], r)
                if n[1] is not None:
                    p1_qT(n[1], 1 - r)
                if n[1] is not None:
                    p1_c(n[1], 1 - r)
                if n[3] is not None:
                    p3_ctx(n[3], 1 - r)
                if n[4] is not None:
                    p4_exp(n[4], r)
                if n[0] is not None:
                    p0_xT(n[0], r)

            run(act, step)

        @block.vector
        def _(dve):
            dve.wait_ge(s["prep_pool"], 2)
            for b in range(2):
                for u in range(2):
                    nc.vector.memset(cbd[u][64 * b:64 * b + 64, 0, b, LAT:LAT + 1], 1.0)
                nc.vector.memset(half36[64 * b:64 * b + 64, b, :], 1.0)
                nc.vector.memset(half5[64 * b:64 * b + 64, :, b, :], 1.0)
                for u in range(2):
                    ins = nc.vector.memset(ctile[u][64 * b:64 * b + 64, b, KROWS:KALL], -1.0)
            ins.then_inc(s["halves"], 1)
            dve.wait_ge(s["bsel4"], 1)
            nc.vector.tensor_reduce(nsel[:], bsel4[:].rearrange("p c b -> p b c"), AX_X, ALU.add).then_inc(s["nsel"], 1)
            dve.wait_ge(s["nsel"], 1)
            nc.vector.tensor_scalar(nselb[:], nsel[:], -1.0, None, ALU.mult).then_inc(s["nselb"], 1)
            dve.wait_ge(s["wvuT"], 1)
            dve.wait_ge(s["prep_pool"], 4)
            for c in range(DC):
                ins = nc.vector.tensor_tensor(vbd[:, c], hmask[:, c].unsqueeze(2).broadcast_to([P, H, LAT]),
                                              wvuT[:, c].unsqueeze(1).broadcast_to([P, H, LAT]), ALU.mult)
            ins.then_inc(s["vbd"], 1)
            dve.wait_ge(s["coef"], 1)
            dve.wait_ge(s["lbT_ps"], 1)
            nc.vector.tensor_scalar(lbT[:], W[0][:, 0:D], coef[:], None, ALU.mult).then_inc(s["lbT"], 1)
            dve.wait_ge(s["cvec_ps"], 1)
            nc.vector.tensor_tensor(cvec[:], W[0][:, 512:1024], bo[:], ALU.add).then_inc(s["cvec"], 1)
            for k in range(DC):
                dve.wait_ge(s["lora_ps"], k + 1)
                dve.wait_ge(s["wT"], k + 1)
                nc.vector.tensor_tensor(weff[:, k], M[k % 2][:], weff[:, k], ALU.add).then_inc(s["weff"], 1)
            dve.wait_ge(s["wmean_ps"], 1)
            for k in range(DC):
                nc.vector.tensor_tensor(weff[:, k], weff[:, k], M[2][:], ALU.subtract).then_inc(s["wcen"], 1)

            def step(r, n):
                def p1_norm(n, u):
                    dve.wait_ge(ld_x[u], nth(n, 1))
                    nc.vector.bn_stats(st1[:], xin[u][:]).then_inc(s["st1"], 1)
                    dve.wait_ge(s["st1"], done(n, u))
                    dve.nop(nofuse=True)
                    nc.vector.bn_aggr(mv1[:], st1[:]).then_inc(s["mv1"], 1)

                def p1_xn(n, u):
                    dve.wait_ge(s["rs1"], done(n, u))
                    if has(n, u, 2):
                        dve.wait_ge(s["xT"], done(n, u, 2))
                    nc.vector.tensor_scalar(xn[u][:], xin[u][:], mv1[:, 0:1], rs1[:, 0:1], ALU.subtract, ALU.mult).then_inc(s["xn"], 1)

                def p1_qc(n, u):
                    dve.wait_ge(s["qc_ps"], done(n, u))
                    if has(n, u, 1):
                        dve.wait_ge(s["qr"], done(n, u, 1))
                        dve.wait_ge(s["qh"], done(n, u, 1))
                    nc.vector.tensor_tensor(qc[:], M[0][:, 0:P + LAT], bqc[:], ALU.add).then_inc(s["qc"], 1)

                def p2_max(n, u, b):
                    dve.wait_ge(s[f"a0_{b}"], done(n, u))
                    if has(n, u, 2):
                        dve.wait_ge(s["ml0"], done(n, u, 2))
                    nc.vector.tensor_reduce(mx0[u][:, b, :], W[b][:].rearrange("p (h k) -> p h k", k=S), AX_X, ALU.max)\
                        .then_inc(s[f"mx0_{b}"], 1)

                def p3_ctx(n, u):
                    dve.wait_ge(s["pv0"], done(n, u))
                    nc.vector.tensor_reduce(pv5[:].rearrange("p h b j -> p h (b j)"),
                                            M[1][:, 0:HP * NPART * 2 * (LAT + 1)].rearrange("p (h k m) -> p h m k", h=HP, k=NPART),
                                            AX_X, ALU.add).then_inc(s["pv5"], 1)
                    pv = pv5[:].rearrange("p h b j -> p b h j")
                    dve.wait_ge(s["pv5"], done(n, u))
                    nc.vector.reciprocal(rden0[:], pv[:, :, :, LAT]).then_inc(s["rden0"], 1)
                    dve.wait_ge(s["rden0"], done(n, u))
                    if has(n, u, 1):
                        dve.wait_ge(s["ctxTb"], done(n, u, 1))
                    nc.vector.tensor_tensor(ctxn[:], pv[:, :, :, 0:LAT],
                                            rden0[:].unsqueeze(3).broadcast_to([P, 2, HP, LAT]), ALU.mult).then_inc(s["ctxn"], 1)

                def p3_low(n, u, k):
                    cols = slice(k * WIDE, (k + 1) * WIDE)
                    dve.wait_ge(s[f"p0h_{k}"], done(n, u))
                    nc.vector.tensor_tensor(p0l[:, cols], p0[:, cols], p0h[:, cols], ALU.subtract).then_inc(s[f"p0l_{k}"], 1)

                def p3_x1(n, u):
                    dve.wait_ge(s["o"], done(n, u))
                    dve.wait_ge(s["x0b"], done(n, u))
                    nc.vector.tensor_tensor(x1[:], M[2][:], x0b[u][:], ALU.add).then_inc(s["x1"], 1)
                    dve.wait_ge(s["x1"], done(n, u))
                    nc.vector.bn_stats(st2[:], x1[:]).then_inc(s["st2"], 1)
                    dve.wait_ge(s["st2"], done(n, u))
                    if has(n, u, 2):
                        dve.wait_ge(s["x2s"], done(n, u, 2))
                    dve.nop(nofuse=True)
                    nc.vector.bn_aggr(mv2[u][:], st2[:]).then_inc(s["mv2"], 1)

                def p4_center(n, u):
                    dve.wait_ge(s["mv2"], done(n, u))
                    if has(n, u, 2):
                        dve.wait_ge(s["skip"], done(n, u, 2))
                        dve.wait_ge(s["xb"], done(n, u, 2))
                    nc.vector.tensor_scalar(x1c[u][:], x1[:], mv2[u][:, 0:1], None, ALU.subtract).then_inc(s["x1c"], 1)

                def p4_max(n, u):
                    dve.wait_ge(s["xa"], done(n, u))
                    if has(n, u, 1):
                        dve.wait_ge(s["ml1"], done(n, u, 1))
                    nc.vector.tensor_reduce(mx1[:].rearrange("p b c -> p (b c)"), W[0][:].rearrange("p (c m) -> p c m", m=CM),
                                            AX_X, ALU.max).then_inc(s["mx1"], 1)

                def p4_expand(n, u):
                    dve.wait_ge(s["mT1"], done(n, u))
                    if has(n, u, 1):
                        dve.wait_ge(s["xb"], done(n, u, 1))
                    nc.vector.tensor_tensor(mexp[:], M[0][:].bitcast(BF16)[0:MROWS, 0:P].unsqueeze(1).broadcast_to([MROWS, DC, P]),
                                            cmask[:], ALU.mult).then_inc(s["mexp"], 1)

                def p4_rmat(n, u):
                    dve.wait_ge(s["rs2"], done(n, u))
                    if has(n, u, 1):
                        dve.wait_ge(s["skip"], done(n, u, 1))
                    nc.vector.scalar_tensor_tensor(rmat[:], wsbd[:], rs2[u][:], identf[:], ALU.mult, ALU.add).then_inc(s["rmat"], 1)

                def p4_x2(n, u):
                    pv = W[0][:].rearrange("p (b m) -> p b m", b=2)[:, :, 0:DC * (CD + 1)].rearrange("p b (c k) -> p b c k", c=DC)
                    dve.wait_ge(s["pv1"], done(n, u))
                    nc.vector.reciprocal(rden1[:], pv[:, :, :, CD]).then_inc(s["rden1"], 1)
                    dve.wait_ge(s["rden1"], done(n, u))
                    for b in range(2):
                        ins = nc.vector.tensor_tensor(pvn[:, :, b, :], pv[:, b, :, 0:CD],
                                                      rden1[:, b, :].unsqueeze(2).broadcast_to([P, DC, CD]), ALU.mult)
                    ins.then_inc(s["pvn"], 1)
                    dve.wait_ge(s["pvn"], done(n, u))
                    dve.wait_ge(s["skip"], done(n, u))
                    if has(n, u, 2):
                        dve.wait_ge(s["ffn"], done(n, u, 2))
                    nc.vector.tensor_tensor(x2T[u][:].rearrange("p c t -> p (c t)"), M[1][:],
                                            pvn[:].rearrange("p c b k -> p (c b k)"), ALU.add).then_inc(s["x2T"], 1)

                def p5_stats(n, u):
                    dve.wait_ge(s["x2s"], done(n, u))
                    nc.vector.bn_stats(st3[:], x2s[:]).then_inc(s["st3"], 1)
                    dve.wait_ge(s["st3"], done(n, u))
                    if has(n, u, 1):
                        dve.wait_ge(s["ve3"], done(n, u, 1))
                    dve.nop(nofuse=True)
                    nc.vector.bn_aggr(mv3[:], st3[:]).then_inc(s["mv3"], 1)

                def p5_y(n, u):
                    dve.wait_ge(s["ffn"], done(n, u))
                    dve.wait_ge(s["rs3"], done(n, u))
                    dve.wait_ge(s["x2b"], done(n, u))
                    if has(n, u, 2):
                        dve.wait_ge(y_out[u], nth(n - 1, 1))
                    nc.vector.scalar_tensor_tensor(y[u][:], M[3][:], rs3[:], x2b[:], ALU.mult, ALU.add).then_inc(s["y"], 1)

                if n[2] is not None:
                    p2_max(n[2], r, 0)
                if n[2] is not None:
                    p2_max(n[2], r, 1)
                if n[4] is not None:
                    p4_center(n[4], r)
                if n[1] is not None:
                    p1_qc(n[1], 1 - r)
                if n[4] is not None:
                    p4_rmat(n[4], r)
                if n[5] is not None:
                    p5_stats(n[5], 1 - r)
                if n[0] is not None:
                    p1_norm(n[0], r)
                if n[4] is not None:
                    p4_max(n[4], r)
                if n[3] is not None:
                    p3_low(n[3], 1 - r, 0)
                if n[0] is not None:
                    p1_xn(n[0], r)
                if n[3] is not None:
                    p3_low(n[3], 1 - r, 1)
                if n[4] is not None:
                    p4_expand(n[4], r)
                if n[3] is not None:
                    p3_ctx(n[3], 1 - r)
                if n[3] is not None:
                    p3_x1(n[3], 1 - r)
                if n[5] is not None:
                    p5_y(n[5], 1 - r)
                if n[4] is not None:
                    p4_x2(n[4], r)

            run(dve, step)

        @block.tensor
        def _(pe):
            mm = nc.tensor.matmul
            tr = nc.tensor.transpose
            pe.wait_ge(s["prep_pool"], 4)
            pe.wait_ge(s["ld_attn"], 96)
            for c in range(DC):
                ins = tr(M[0][0:QL, c * P:(c + 1) * P], wqd[:, c], identf[:])
            ins.then_inc(s["wqdT_ps"], 1)
            pe.wait_ge(s["ld_vo"], 64)
            pe.wait_ge(s["ld_ffn"], 128)
            for c in range(DC):
                ins = tr(M[1][:, c * LAT:(c + 1) * LAT], wvu[:, c * P:(c + 1) * P], identf[0:LAT, 0:LAT])
            ins = tr(M[1][:, DC * LAT:DC * LAT + DC], bvr[:], identf[0:DC, 0:DC])
            ins.then_inc(s["wvuT_ps"], 1)
            pe.wait_ge(s["w13p"], 1)
            mm(M[1][:, 128:128 + P], bq13[:].broadcast_to([QL + 1, P]), w13p[:], start=True, stop=True)
            mm(M[1][:, 33:34], spread[:], lw[:], start=True, stop=True).then_inc(s["cols_ps"], 1)
            pe.wait_ge(s["wqdT"], 1)
            for c in range(DC):
                ins = mm(M[0][:, c * P:(c + 1) * P], wqdT[:, c * P:(c + 1) * P], w13p[0:QL, :], start=True, stop=True)
            ins.then_inc(s["wqc_ps"], 1)
            pe.wait_ge(s["ld_x"], 112)
            mm(M[2][:, 0:CD], xwk[:].rearrange("p a b -> p (a b)"), xwq[:], start=True, stop=True)
            tr(M[2][:, 64:128], xwv[:].rearrange("p a b -> p (a b)"), identf[0:CD, 0:CD])
            tr(M[2][:, 128:192], xws[:].rearrange("p a b -> p (a b)"), identf[0:CD, 0:CD]).then_inc(s["xw_ps"], 1)
            for c in range(DC):
                ins = tr(W[0][:, c * P:(c + 1) * P], lb[:, c].rearrange("p n r -> p (n r)"), identf[:])
            ins.then_inc(s["lbT_ps"], 1)
            pe.wait_ge(s["vbd"], 1)
            for c in range(DC):
                ins = mm(M[3][:], vbd[:, c].rearrange("p h j -> p (h j)"), wo[:, c], start=(c == 0), stop=(c == DC - 1))
            ins.then_inc(s["mout_ps"], 1)
            for c in range(DC):
                ins = mm(W[0][:, 512:1024], bvT[:, c:c + 1].broadcast_to([P, P]), wo[:, c], start=(c == 0), stop=(c == DC - 1))
            ins.then_inc(s["cvec_ps"], 1)
            pe.wait_ge(s["cvec"], 1)
            for k in range(DC):
                for c in range(DC):
                    ins = tr(W[k // 2][:, (k % 2) * 512 + c * P:(k % 2) * 512 + (c + 1) * P], fw[:, c, k * P:(k + 1) * P], identf[:])
                ins.then_inc(s["wT_ps"], 1)
            pe.wait_ge(s["wqc"], 1)
            for k in range(DC):
                if k >= 2:
                    pe.wait_ge(s["weff"], k - 1)
                mm(M[k % 2][:], la[:, k * P:(k + 1) * P], lbT[:], start=True, stop=True).then_inc(s["lora_ps"], 1)
            pe.wait_ge(s["xw"], 1)
            pe.wait_ge(s["weff"], DC)
            for k in range(DC):
                ins = mm(M[2][:], meanw[:], weff[:, k], start=(k == 0), stop=(k == DC - 1))
            ins.then_inc(s["wmean_ps"], 1)
            pe.wait_ge(s["wcen"], DC)

            def step(r, n):
                def p0_xT(n, u):
                    pe.wait_ge(s["xn"], done(n, u))
                    if has(n, u, 4):
                        pe.wait_ge(s["mexp"], done(n, u, 4))
                    elif has(n, u, 1):
                        pe.wait_ge(s["cst"], done(n, u, 1))
                    for c in range(DC):
                        ins = tr(M[0][:, c * P:(c + 1) * P], xn[u][:, c * P:(c + 1) * P], identf[:])
                    ins.then_inc(s["xT"], 1)

                def p1_qc(n, u):
                    pe.wait_ge(s["xnT"], done(n, u))
                    for c in range(DC):
                        ins = mm(M[0][:, 0:P + LAT], xnT[:, c], wqc[:, c], start=(c == 0), stop=(c == DC - 1))
                    ins.then_inc(s["qc_ps"], 1)

                def p1_cT(n, u):
                    pe.wait_ge(s["ql"], done(n, u))
                    for k in range(NPART):
                        ins = tr(M[0][:].bitcast(BF16)[:, (1 + k) * P:(2 + k) * P], qcp[:, k, 0:P], ident[:])
                    ins.then_inc(s["qT"], 1)
                    pe.wait_ge(s["ctile"], done(n, u))
                    tr(M[0][:].bitcast(BF16)[:, 0:P], ctile[u][:].rearrange("p b k -> p (b k)"), ident[:]).then_inc(s["cstT"], 1)

                def p2_scores(n, u, b):
                    if has(n, u, 3):
                        pe.wait_ge(s["pvn" if b == 0 else "e1"], done(n, u, 3))
                    elif has(n, u, 2):
                        pe.wait_ge(s[f"e0_{b}"], done(n, u, 2))
                    elif has(n, u, 1):
                        pe.wait_ge(s[f"mx0_{b}"], done(n, u, 1))
                    pe.wait_ge(q_in[u], nth(n, 6))
                    pe.wait_ge(s["cst"], done(n, u))
                    rows = slice(64 * b, 64 * b + KROWS)
                    for h in range(HP):
                        ins = mm(W[b][:, h * S:(h + 1) * S], qst[u][rows, h * P:(h + 1) * P], cst[u][rows, 64 * b:64 * b + 64],
                                 start=True, stop=True)
                    ins.then_inc(s[f"a0_{b}"], 1)

                def p2_maxT(n, u):
                    if has(n, u, 3):
                        pe.wait_ge(s["x2T"], done(n, u, 3))
                    elif has(n, u, 2):
                        pe.wait_ge(s["ctx_lo"], done(n, u, 2))
                    elif has(n, u, 1):
                        pe.wait_ge(s["mx0T"], done(n, u, 1))
                    pe.wait_ge(s["ml0"], done(n, u))
                    tr(M[1][:].bitcast(BF16)[0:2 * NPART * HP, 0:P], mp0[:].rearrange("p b a h -> p (b a h)"), ident[:])\
                        .then_inc(s["mT0"], 1)

                def p3_scores(n, u, k):
                    if not last(n, u):
                        pe.wait_ge(s[f"mx0_{k}"], done(n, u, -1))
                    else:
                        pe.wait_ge(s["pvn" if k == 0 else "e1"], done(n, u, 2))
                    pe.wait_ge(m_in[u], nth(n, 2))
                    for c in range(2):
                        col = k * WIDE + c * 512
                        ins = mm(W[k][:, c * 512:(c + 1) * 512], cst[u][0:64 + KALL, :], qst[u][0:64 + KALL, col:col + 512],
                                 start=True, stop=True)
                    ins.then_inc(s[f"b0_{k}"], 1)

                def p3_values(n, u):
                    if not last(n, u):
                        pe.wait_ge(s["mx0T"], done(n, u, -1))
                    else:
                        pe.wait_ge(s["x2T"], done(n, u, 2))
                    pe.wait_ge(s["cbd"], done(n, u))
                    width = NPART * 2 * (LAT + 1)
                    for h in range(HP):
                        if h % (HP // 2) == 0:
                            pe.wait_ge(s[f"p0l_{h // (HP // 2)}"], done(n, u))
                        for part in (p0h, p0l):
                            ins = mm(M[1][:, h * width:(h + 1) * width], part[:, h * P:(h + 1) * P],
                                     cbd[u][:].rearrange("p k b j -> p (k b j)"), start=(part is p0h), stop=(part is p0l))
                    ins.then_inc(s["pv0"], 1)

                def p3_ctxT(n, u):
                    pe.wait_ge(s["ctxn"], done(n, u))
                    if has(n, u, 1):
                        pe.wait_ge(s["v"], done(n, u, 1))
                    pe.nop(nofuse=True)
                    for k in range(2):
                        rows = slice(64 * k, 64 * k + 64)
                        for b in range(2):
                            ins = mm(M[1 + k][rows, b * 64:b * 64 + 64], ctxn[rows, b].rearrange("p h j -> p (h j)"),
                                     identf[rows, 64 * k:64 * k + 64], start=True, stop=True)
                        ins.then_inc(s["ctxTa" if k == 0 else "ctxTb"], 1)

                def p3_out(n, u):
                    pe.wait_ge(s["ctx_lo"], done(n, u))
                    pe.wait_ge(s["ctx_hi"], done(n, u))
                    mm(M[2][:], ctxT[:], mout[:], start=True, stop=True).then_inc(s["o"], 1)

                def p4_gv(n, u):
                    pe.wait_ge(s["x1"], done(n, u))
                    pe.wait_ge(ld_c[u], nth(n, 1))
                    mm(M[2][:, 0:CM], kq[:], cin[u][:], start=True, stop=True)
                    mm(M[2][:, CM:CM + P], cin[u][:], wvbd[:], start=True, stop=True).then_inc(s["gv"], 1)

                def p4_a(n, u):
                    if not last(n, u):
                        pe.wait_ge(s["e0_0"], done(n, u, -1))
                    else:
                        pe.wait_ge(s["pvn"], done(n, u, 1))
                    pe.wait_ge(s["g"], done(n, u))
                    pe.wait_ge(s["x1c"], done(n, u))
                    for b in range(2):
                        rows = slice(64 * b, 64 * b + 64)
                        for c in range(DC):
                            col = b * 512 + c * P
                            ins = mm(W[0][:, col:col + P], x1c[u][rows, c * P:(c + 1) * P], g[rows, :], start=True, stop=True)
                    ins.then_inc(s["xa"], 1)

                def p4_b(n, u):
                    if not last(n, u):
                        pe.wait_ge(s["e0_1"], done(n, u, -1))
                    else:
                        pe.wait_ge(s["e1"], done(n, u, 1))
                    for b in range(2):
                        rows = slice(64 * b, 64 * b + 64)
                        mm(W[1][:, b * 512:(b + 1) * 512], g[rows, :], x1c[u][rows, :], start=True, stop=False)

                def p4_bmax(n, u):
                    pe.wait_ge(s["mexp"], done(n, u))
                    for b in range(2):
                        ins = mm(W[1][:, b * 512:(b + 1) * 512], nselb[:, b:b + 1].broadcast_to([MROWS, P]),
                                 mexp[:].rearrange("p c n -> p (c n)"), start=False, stop=True)
                    ins.then_inc(s["xb"], 1)

                def p4_maxT(n, u):
                    if not last(n, u, 3):
                        pe.wait_ge(s["cst"], done(n, u, -3))
                    else:
                        pe.wait_ge(s["mexp"], done(n, u, 1))
                    pe.wait_ge(s["ml1"], done(n, u))
                    tr(M[0][:].bitcast(BF16)[0:MROWS, 0:P], mp1[:].rearrange("p c b k -> p (c b k)"), ident[:]).then_inc(s["mT1"], 1)

                def p4_skip(n, u):
                    if not last(n, u):
                        pe.wait_ge(s["ctx_lo"], done(n, u, -1))
                    else:
                        pe.wait_ge(s["x2T"], done(n, u, 1))
                    pe.wait_ge(s["rmat"], done(n, u))
                    for c in range(DC):
                        ins = mm(M[1][:, c * P:(c + 1) * P], x1c[u][:, c * P:(c + 1) * P], rmat[:], start=True, stop=True)
                    ins.then_inc(s["skip"], 1)

                def p4_values(n, u):
                    pe.wait_ge(s["e1"], done(n, u))
                    pe.wait_ge(s["mx1"], done(n, u))
                    pe.wait_ge(s["v"], done(n, u))
                    for b in range(2):
                        for c in range(DC):
                            col = b * 512 + c * (CD + 1)
                            ins = mm(W[0][:, col:col + CD + 1], pt[:, b, c * P:(c + 1) * P], v65[u][:, b, :], start=True, stop=True)
                    ins.then_inc(s["pv1"], 1)

                def p5_x2(n, u):
                    pe.wait_ge(s["x2T"], done(n, u))
                    if has(n, u, 1):
                        pe.wait_ge(s["y"], done(n, u, 1))
                    for c in range(DC):
                        ins = tr(M[3][:, c * P:(c + 1) * P], x2T[u][:, c, :], identf[:])
                    ins.then_inc(s["x2"], 1)

                def p5_ffn(n, u, half):
                    if half == 0:
                        pe.wait_ge(s["x2s"], done(n, u))
                    for c in range(half * DC // 2, (half + 1) * DC // 2):
                        ins = mm(M[3][:], x2T[u][:, c, :], weff[:, c], start=(c == 0), stop=(c == DC - 1))
                    if half == 1:
                        ins.then_inc(s["ffn"], 1)

                if n[4] is not None:
                    p4_gv(n[4], r)
                if n[2] is not None:
                    p2_scores(n[2], r, 1)
                if n[2] is not None:
                    p2_scores(n[2], r, 0)
                if n[5] is not None:
                    p5_x2(n[5], 1 - r)
                if n[3] is not None:
                    p3_scores(n[3], 1 - r, 0)
                if n[1] is not None:
                    p1_qc(n[1], 1 - r)
                if n[3] is not None:
                    p3_scores(n[3], 1 - r, 1)
                if n[4] is not None:
                    p4_a(n[4], r)
                if n[2] is not None:
                    p2_maxT(n[2], r)
                if n[1] is not None:
                    p1_cT(n[1], 1 - r)
                if n[4] is not None:
                    p4_b(n[4], r)
                if n[5] is not None:
                    p5_ffn(n[5], 1 - r, 0)
                if n[4] is not None:
                    p4_maxT(n[4], r)
                if n[3] is not None:
                    p3_values(n[3], 1 - r)
                if n[5] is not None:
                    p5_ffn(n[5], 1 - r, 1)
                if n[4] is not None:
                    p4_bmax(n[4], r)
                if n[3] is not None:
                    p3_ctxT(n[3], 1 - r)
                if n[0] is not None:
                    p0_xT(n[0], r)
                if n[3] is not None:
                    p3_out(n[3], 1 - r)
                if n[4] is not None:
                    p4_skip(n[4], r)
                if n[4] is not None:
                    p4_values(n[4], r)

            run(pe, step)


_INS = ["x", "ctx_1024", "L0_attn_Wq_d", "L0_attn_bq_d", "L0_attn_W_qk", "L0_attn_b_qk", "L0_attn_Wkv_d",
        "L0_attn_bkv_d", "L0_attn_Wv_u", "L0_attn_bv_u", "L0_attn_Wo", "L0_attn_bo", "L0_xattn_Wq", "L0_xattn_Wk",
        "L0_xattn_Wv", "L0_xattn_Wskip", "L0_ffn_lora_A", "L0_ffn_lora_B", "L0_ffn_W", "L0_ffn_bias",
        "L0_ffn_lora_weights"]


def kernel(**inputs):
    import numpy as _np
    import concourse.bacc as _bacc
    from concourse import mybir as _mybir
    from concourse.bass_utils import run_bass_kernel_spmd as _run

    nc = _bacc.Bacc("TRN2", target_bir_lowering=False, num_devices=1)
    arrays, io = {}, {}
    for name in _INS:
        a = _np.ascontiguousarray(inputs[name])
        arrays[f"in_{name}"] = a
        io[name] = nc.dram_tensor(f"in_{name}", a.shape, _mybir.dt.from_np(a.dtype), kind="ExternalInput").ap()
    io["out"] = nc.dram_tensor("out_y", inputs["x"].shape, _mybir.dt.float32, kind="ExternalOutput").ap()
    decoder(nc, io)
    r = _run(nc, [arrays], core_ids=[0])
    return r.results[0]["out_y"]
```

```python
from contextlib import ExitStack

import concourse.bass as bass
from concourse import mybir

F32 = mybir.dt.float32
BF16 = mybir.dt.bfloat16
F16 = mybir.dt.float16
ALU = mybir.AluOpType
ACT = mybir.ActivationFunctionType
AX_X = mybir.AxisListType.X

P = 128
B, S, D = 32, 64, 512
PAIRS = B * S // P
DC = D // P
H, LAT, QL = 32, 4, 12
HP = H // 2
HD = D // H
CD, CM = S, P
NL, RANK, ALPHA = 8, 16, 32
EPS = 1e-5
NPART = 3
KROWS = NPART * NPART * LAT
KALL = KROWS + NPART
LN_TOP = 15 * 0.6931471805599453
WIDE = 2 * 512


def done(n, u, back=0):
    return 2 * n + (u + 1 - back)


def decoder(nc, io):
    x_d = io["x"].rearrange("b s d -> (b s) d")
    ctx_d = io["ctx_1024"].rearrange("b c m -> (b c) m")
    out_d = io["out"].rearrange("b s d -> (b s) d")
    es = ExitStack()
    with es:
        def sb(name, shape, dt=F32):
            return es.enter_context(nc.sbuf_tensor(name, shape, dt))

        def sem(name):
            return es.enter_context(nc.semaphore(name))

        identf = sb("identf", [P, P])
        ident = sb("ident", [P, P], BF16)
        half36 = sb("half36", [P, 2, KROWS], BF16)
        half5 = sb("half5", [P, NPART, 2, LAT], BF16)
        mhalf = sb("mhalf", [P, 1])
        epsc = sb("epsc", [P, 1])
        minus1 = sb("minus1", [P, 1])
        nscale = sb("nscale", [P, 2, DC])
        ones = sb("ones", [P, P])
        meanw = sb("meanw", [P, P])
        wqd = sb("wqd", [P, DC, QL])
        w13 = sb("w13", [QL + 1, P])
        w13p = sb("w13p", [QL + 1, P])
        bq13 = sb("bq13", [QL + 1, 1])
        wqdT = sb("wqdT", [QL, D])
        wqc = sb("wqc", [P, DC, P + LAT])
        bqc = sb("bqc", [P, P + LAT])
        wvu = sb("wvu", [LAT, D])
        vT = sb("vT", [P, DC * LAT + DC])
        wvuT = vT[:, 0:DC * LAT].rearrange("p (c j) -> p c j", j=LAT)
        hmask = sb("hmask", [P, DC, H])
        vbd = sb("vbd", [P, DC, H, LAT])
        wo = sb("wo", [P, DC, D])
        bvr = sb("bvr", [DC, P])
        bvT = vT[:, DC * LAT:DC * LAT + DC]
        bo = sb("bo", [P, D])
        mout = sb("mout", [P, D])
        cvec = sb("cvec", [P, D])
        xwk = sb("xwk", [CD, 2, CD])
        xwq = sb("xwq", [CD, CD])
        xwv = sb("xwv", [CD, 2, CD])
        xws = sb("xws", [CD, 2, CD])
        kq = sb("kq", [P, P])
        wvbd = sb("wvbd", [P, P])
        wsbd = sb("wsbd", [P, P])
        fw = sb("fw", [P, DC, D])
        la = sb("la", [P, D])
        lb = sb("lb", [P, DC, NL, RANK])
        lbT = sb("lbT", [P, D])
        lw = sb("lw", [NL, 1])
        spread = sb("spread", [NL, P])
        coef = sb("coef", [P, 1])
        weff = sb("weff", [P, DC, D])
        fbias = sb("fbias", [P, D])

        def two(name, shape, dt=F32):
            return [sb(f"{name}{u}", shape, dt) for u in range(2)]

        xin = two("xin", [P, D])
        st1 = sb("st1", [P, 6])
        mv1 = sb("mv1", [P, 2])
        rs1 = sb("rs1", [P, 2])
        xn = two("xn", [P, D])
        x0b = two("x0b", [P, D])
        xnT = sb("xnT", [P, DC, P])
        qc = sb("qc", [P, P + LAT])
        qr = sb("qr", [P, P + LAT])
        qcp = sb("qcp", [P, NPART, P + LAT], BF16)
        qpart = two("qpart", [P, 2, NPART, S], BF16)
        ctile = two("ctile", [P, 2, S], BF16)
        cbd = two("cbd", [P, NPART, 2, LAT + 1], BF16)
        cst = two("cst", [P, P], BF16)
        qst = two("qst", [P, H * S], BF16)
        mx0 = two("mx0", [P, 2, HP])
        mr0 = sb("mr0", [P, 2, HP])
        mp0 = sb("mp0", [P, 2, NPART, HP], BF16)
        mx0T = two("mx0T", [2 * NPART * HP, P], BF16)
        p0 = sb("p0", [P, H * S])
        p0h = sb("p0h", [P, H * S], F16)
        p0l = sb("p0l", [P, H * S], F16)
        pv5 = sb("pv5", [P, HP, 2, LAT + 1])
        lntop = sb("lntop", [P, 1])
        rden0 = sb("rden0", [P, 2, HP])
        ctxn = sb("ctxn", [P, 2, HP, LAT])
        ctxT = sb("ctxT", [P, P])
        x1 = sb("x1", [P, D])
        st2 = sb("st2", [P, 6])
        mv2 = two("mv2", [P, 2])
        nmean2 = sb("nmean2", [P, 1])
        ve2 = sb("ve2", [P, 1])
        rs2 = two("rs2", [P, 1])
        x1c = two("x1c", [P, D])
        cin = two("cin", [P, CM])
        g = sb("g", [P, CM])
        v65 = two("v65", [P, 2, CD + 1])
        mx1 = sb("mx1", [P, 2, DC])
        nmx1 = sb("nmx1", [P, 2, DC])
        ex = sb("ex", [P, 2, D])
        pt = sb("pt", [P, 2, D])
        rmat = sb("rmat", [P, P])
        rden1 = sb("rden1", [P, 2, DC])
        pvn = sb("pvn", [P, DC, 2, CD])
        x2T = two("x2T", [P, DC, P])
        st3 = sb("st3", [P, 6])
        mv3 = sb("mv3", [P, 2])
        ve3 = sb("ve3", [P, 1])
        rs3 = sb("rs3", [P, 1])
        x2s = sb("x2s", [P, D])
        x2b = sb("x2b", [P, D])
        y = two("y", [P, D])

        q_scr = [nc.dram_tensor(f"q_scr{u}", (2 * NPART, P, S), BF16, kind="Internal").ap() for u in range(2)]
        m_scr = [nc.dram_tensor(f"m_scr{u}", (2 * NPART * HP, P), BF16, kind="Internal").ap() for u in range(2)]

        W = [es.enter_context(nc.psum_tensor(f"wide{k}", [P, WIDE], F32)) for k in range(2)]
        M = [es.enter_context(nc.psum_tensor(f"bank{k}", [P, 512], F32)) for k in range(4)]

        names = """ld_wqd ld_qk ld_attn ld_vu ld_vo ld_x ld_ffn bq_one zeros halves masks1 masks2 identf ident w13p
        wqdT_ps wqdT bqc_ps bqc wqc_ps wqc wvuT_ps wvuT xw_ps xw vbd mout_ps mout cvec_ps cvec
        coef_ps coef lbT_ps lbT wT_ps wT wmean_ps wcen
        st1 mv1 ve1 rs1 xn xT xnT x0b qc_ps qc qh qr qm ql cbd ctile qT qpart cstT cst
        a0_0 a0_1 mx0_0 mx0_1 mh0 mr0 mm0 ml0 mT0 mx0T b0_0 b0_1 e0_0 e0_1 p0h_0 p0h_1 p0l_0 p0l_1 p0l_pool
        pv5 pv0 rden0 ctxn ctxTa ctxTb ctx_lo ctx_hi
        o x1 st2 mv2 ve2 rs2 nmean2 x1c gv g v xa mx1 nmx1 ex_0 ex_1 pT e1 rmat skip pv1 rden1 pvn x2T
        x2 st3 mv3 ve3 rs3 x2s ffn x2b y ffn_half y_half"""
        s = {n: sem("s_" + n) for n in names.split()}
        ld_x = [sem(f"s_xin{u}") for u in range(2)]
        ld_c = [sem(f"s_cin{u}") for u in range(2)]
        q_out = [sem(f"s_qout{u}") for u in range(2)]
        q_in = [[sem(f"s_qin{u}_{b}") for b in range(2)] for u in range(2)]
        m_out = [sem(f"s_mout{u}") for u in range(2)]
        m_in = [sem(f"s_min{u}") for u in range(2)]
        y_out = [sem(f"s_stored{u}") for u in range(2)]
        last_out = sem("s_stored_last")

        PHASES = 6
        FIRST = PHASES + 2

        def run(eng, step, prepare):
            def pairs(i):
                return [(i - k) // 2 if 0 <= i - k < PAIRS else None for k in range(PHASES)]
            for i in range(FIRST):
                if i in prepare:
                    prepare[i]()
                step(i % 2, pairs(i))
            with eng.Fori(FIRST // 2, PAIRS // 2) as j:
                for r in range(2):
                    step(r, [j + (r - k) // 2 if (r - k) // 2 else j for k in range(PHASES)])
            for i in range(PAIRS, PAIRS + PHASES - 1):
                step(i % 2, pairs(i))

        def has(n, u, back):
            return not isinstance(n, int) or 2 * n + u >= back

        def last(n, u, ahead=1):
            return isinstance(n, int) and 2 * n + u + ahead >= PAIRS

        def half_of(k):
            return slice(k * D // 2, (k + 1) * D // 2), slice(k * 512, k * 512 + D // 2)

        def nth(n, k):
            return n * (16 * k) + 16 * k

        block = es.enter_context(nc.Block())

        @block.sync
        def _(sp):
            sp.dma_start(wqd[:], io["L0_attn_Wq_d"].rearrange("(c p) k -> p c k", p=P)).then_inc(s["ld_wqd"], 16)
            sp.dma_start(w13[0:QL, :], io["L0_attn_W_qk"]).then_inc(s["ld_qk"], 16)
            sp.dma_start(w13[QL:QL + 1, :], io["L0_attn_b_qk"].rearrange("(a n) -> a n", a=1)).then_inc(s["ld_qk"], 16)
            sp.wait_ge(s["bq_one"], 1)
            sp.dma_start(bq13[0:QL, :], io["L0_attn_bq_d"].rearrange("(n a) -> n a", a=1)).then_inc(s["ld_attn"], 16)
            sp.dma_start(wqc[:, :, P:P + LAT], io["L0_attn_Wkv_d"].rearrange("(c p) k -> p c k", p=P)).then_inc(s["ld_attn"], 16)
            sp.dma_start(bqc[:, P:P + LAT],
                         io["L0_attn_bkv_d"].rearrange("(a n) -> a n", a=1).broadcast_to([P, LAT])).then_inc(s["ld_attn"], 16)
            sp.dma_start(wo[:], io["L0_attn_Wo"].rearrange("(c p) n -> p c n", p=P)).then_inc(s["ld_vo"], 16)
            sp.dma_start(bo[:], io["L0_attn_bo"].rearrange("(a n) -> a n", a=1).broadcast_to([P, D])).then_inc(s["ld_vo"], 16)
            sp.dma_start(xwq[:], io["L0_xattn_Wq"]).then_inc(s["ld_x"], 16)
            for k in range(2):
                sp.dma_start(xwk[:, k, :], io["L0_xattn_Wk"]).then_inc(s["ld_x"], 16)
                sp.dma_start(xwv[:, k, :], io["L0_xattn_Wv"]).then_inc(s["ld_x"], 16)
                sp.dma_start(xws[:, k, :], io["L0_xattn_Wskip"]).then_inc(s["ld_x"], 16)
            sp.dma_start(lw[:], io["L0_ffn_lora_weights"].rearrange("(n a) -> n a", a=1)).then_inc(s["ld_ffn"], 16)
            for c in range(DC):
                sp.dma_start(lb[:, c], io["L0_ffn_lora_B"][:, c * P:(c + 1) * P, :].rearrange("n p r -> p n r")).then_inc(s["ld_ffn"], 16)
            sp.dma_start(la[:], io["L0_ffn_lora_A"].rearrange("n r d -> (n r) d")).then_inc(s["ld_ffn"], 16)
            sp.dma_start(fw[:], io["L0_ffn_W"].rearrange("(c p) n -> p c n", p=P)).then_inc(s["ld_ffn"], 16)
            sp.dma_start(fbias[:], io["L0_ffn_bias"].rearrange("(a n) -> a n", a=1).broadcast_to([P, D])).then_inc(s["ld_ffn"], 16)

            def step(r, n):
                def p0_load(n, u):
                    if not has(n, u, 2):
                        return
                    sp.wait_ge(s["xn"], done(n, u, 2))
                    sp.nop(nofuse=True)
                    sp.wait_ge(s["x0b"], done(n, u, 2))
                    sp.nop(nofuse=True)
                    sp.dma_start(xin[u][:], x_d[bass.ds((n * 2 + u) * P, P), :]).then_inc(ld_x[u], 16)

                def p2_out(n, u):
                    sp.wait_ge(s["mx0T"], done(n, u))
                    sp.nop(nofuse=True)
                    sp.dma_start(m_scr[u], mx0T[u][:]).then_inc(m_out[u], 16)

                def p2_in(n, u):
                    sp.wait_ge(m_out[u], nth(n, 1))
                    sp.nop(nofuse=True)
                    for b in range(2):
                        sp.dma_start(qst[u][64 * b + KROWS:64 * b + KALL, :],
                                     m_scr[u].rearrange("(b a h) q -> b a (h q)", b=2, a=NPART)[b]).then_inc(m_in[u], 16)

                def p1_out(n, u):
                    if has(n, u, 2):
                        for b in range(2):
                            sp.wait_ge(q_in[u][b], nth(n - 1, 3))
                            sp.nop(nofuse=True)
                    sp.wait_ge(s["qpart"], done(n, u))
                    sp.nop(nofuse=True)
                    sp.dma_start(q_scr[u].rearrange("k p q -> p k q"),
                                 qpart[u][:].rearrange("p b a q -> p (b a) q")).then_inc(q_out[u], 16)

                def p1_in(n, u):
                    sp.wait_ge(q_out[u], nth(n, 1))
                    sp.nop(nofuse=True)
                    if has(n, u, 2):
                        sp.wait_ge(s["b0_0"], done(n, u, 2))
                        sp.nop(nofuse=True)
                    for b in (1, 0):
                        rows = q_scr[u][NPART * b:NPART * (b + 1)].rearrange("a (j h) q -> (a j) (h q)", j=LAT)
                        for part in range(NPART):
                            r0 = 64 * b + part * NPART * LAT
                            sp.dma_start(qst[u][r0:r0 + NPART * LAT, :], rows).then_inc(q_in[u][b], 16)

                def p5_store(n, u):
                    sp.wait_ge(s["y"], done(n, u))
                    sp.nop(nofuse=True)
                    sp.dma_start(out_d[bass.ds((n * 2 + u) * P, P), :], y[u][:]).then_inc(y_out[u], 16)

                def p5_store_halves(n, u):
                    for k in range(2):
                        cols, _ = half_of(k)
                        sp.wait_ge(s["y_half"], k + 1)
                        sp.nop(nofuse=True)
                        sp.dma_start(out_d[(n * 2 + u) * P:(n * 2 + u + 1) * P, cols], y[u][:, cols]).then_inc(last_out, 16)

                if n[0] is not None:
                    p0_load(n[0], r)
                if n[1] is not None:
                    p1_out(n[1], 1 - r)
                if n[2] is not None:
                    p2_out(n[2], r)
                if n[1] is not None:
                    p1_in(n[1], 1 - r)
                if n[2] is not None:
                    p2_in(n[2], r)
                if n[5] is not None and last(n[5], 1 - r):
                    p5_store_halves(n[5], 1 - r)
                elif n[5] is not None:
                    p5_store(n[5], 1 - r)

            run(sp, step, {})
            sp.wait_ge(y_out[0], nth(PAIRS // 2 - 1, 1))
            sp.wait_ge(y_out[1], nth(PAIRS // 2 - 2, 1))
            sp.wait_ge(last_out, 16 * 2)

        @block.gpsimd
        def _(pool):
            nc.gpsimd.memset(bq13[:], 1.0).then_inc(s["bq_one"], 1)
            nc.gpsimd.memset(identf[:], 0.0)
            nc.gpsimd.memset(mhalf[:], -0.5)
            nc.gpsimd.memset(epsc[:], EPS)
            nc.gpsimd.memset(minus1[:], -1.0)
            nc.gpsimd.memset(nscale[:], -float(CD) ** -0.5)
            nc.gpsimd.memset(lntop[:], LN_TOP)
            nc.gpsimd.memset(ones[:], 1.0)
            nc.gpsimd.memset(meanw[:], 1.0 / D).then_inc(s["masks1"], 1)
            pool.wait_ge(s["masks1"], 1)
            nc.gpsimd.affine_select(out=identf[:], in_=identf[:], compare_op=ALU.not_equal, fill=1.0, base=0,
                                    pattern=[[-1, P]], channel_multiplier=1).then_inc(s["identf"], 1)
            nc.gpsimd.memset(spread[:], 1.0)
            nc.gpsimd.memset(hmask[:], 1.0).then_inc(s["masks1"], 1)
            pool.wait_ge(s["identf"], 1)
            nc.gpsimd.tensor_copy(ident[:], identf[:]).then_inc(s["ident"], 1)
            pool.wait_ge(s["ld_qk"], 32)
            nc.gpsimd.tensor_copy(w13p[:].rearrange("c (j h) -> c j h", j=LAT),
                                  w13[:].rearrange("c (h j) -> c j h", j=LAT)).then_inc(s["w13p"], 1)

            def masks():
                pool.wait_ge(s["masks1"], 2)
                nc.gpsimd.affine_select(out=hmask[:], in_=hmask[:], compare_op=ALU.is_ge, fill=0.0, base=0,
                                        pattern=[[P, DC], [-HD, 2], [-2 * HD, HP]], channel_multiplier=1)
                nc.gpsimd.affine_select(out=spread[:], in_=spread[:], compare_op=ALU.is_ge, fill=0.0, base=0,
                                        pattern=[[1, P]], channel_multiplier=-RANK).then_inc(s["masks1"], 1)
                pool.wait_ge(s["masks1"], 3)
                nc.gpsimd.affine_select(out=hmask[:], in_=hmask[:], compare_op=ALU.is_ge, fill=0.0, base=HD - 1,
                                        pattern=[[-P, DC], [HD, 2], [2 * HD, HP]], channel_multiplier=-1)
                nc.gpsimd.affine_select(out=spread[:], in_=spread[:], compare_op=ALU.is_ge, fill=0.0, base=RANK - 1,
                                        pattern=[[-1, P]], channel_multiplier=RANK).then_inc(s["masks2"], 1)
                pool.wait_ge(s["halves"], 1)

            def rstd(ve, var, out, wait_var, ve_done, rs_done, n, u):
                pool.wait_ge(s[wait_var], done(n, u))
                nc.gpsimd.tensor_tensor(ve, var, epsc[:], ALU.add).then_inc(s[ve_done], 1)
                pool.wait_ge(s[ve_done], done(n, u))
                nc.gpsimd.tensor_tensor(out, ve, mhalf[:], ALU.pow).then_inc(s[rs_done], 1)

            def step(r, n):
                def p0_rstd(n, u):
                    rstd(rs1[:, 1:2], mv1[:, 1:2], rs1[:, 0:1], "mv1", "ve1", "rs1", n, u)

                def p1_residual(n, u):
                    if not has(n, u, 1):
                        pool.wait_ge(s["cvec"], 1)
                    if has(n, u, 2):
                        pool.wait_ge(s["x1"], done(n, u, 2))
                    pool.wait_ge(ld_x[u], nth(n, 1))
                    nc.gpsimd.tensor_tensor(x0b[u][:], xin[u][:], cvec[:], ALU.add).then_inc(s["x0b"], 1)

                def p1_q(n, u):
                    one = ones[:, 0:1].broadcast_to([P, P + LAT])
                    pool.wait_ge(s["qh"], done(n, u))
                    if has(n, u, 1):
                        pool.wait_ge(s["qT"], done(n, u, 1))
                    nc.gpsimd.tensor_tensor(qr[:], qc[:], qcp[:, 0, :], ALU.subtract).then_inc(s["qr"], 1)
                    pool.wait_ge(s["qr"], done(n, u))
                    nc.gpsimd.tensor_tensor(qcp[:, 1, :], qr[:], one, ALU.mult).then_inc(s["qm"], 1)
                    pool.wait_ge(s["qm"], done(n, u))
                    nc.gpsimd.tensor_tensor(qcp[:, 2, :], qr[:], qcp[:, 1, :], ALU.subtract).then_inc(s["ql"], 1)
                    if has(n, u, 2):
                        pool.wait_ge(s["cstT"], done(n, u, 2))
                    pool.wait_ge(s["ql"], done(n, u))
                    for b in range(2):
                        ins = nc.gpsimd.tensor_tensor(
                            ctile[u][:, b, 0:KROWS].rearrange("p (k a j) -> p k a j", k=NPART, a=NPART),
                            qcp[:, :, P:P + LAT].unsqueeze(2).broadcast_to([P, NPART, NPART, LAT]),
                            half36[:, b, :].rearrange("p (k a j) -> p k a j", k=NPART, a=NPART), ALU.mult)
                    ins.then_inc(s["ctile"], 1)

                def p1_values(n, u):
                    if has(n, u, 2):
                        pool.wait_ge(s["pv0"], done(n, u, 2))
                    for b in range(2):
                        ins = nc.gpsimd.tensor_tensor(cbd[u][:, :, b, 0:LAT], qcp[:, :, P:P + LAT], half5[:, :, b, :], ALU.mult)
                    ins.then_inc(s["cbd"], 1)

                def p2_split(n, u):
                    one = ones[:, 0:2 * HP].rearrange("p (b h) -> p b h", b=2)
                    if has(n, u, 1):
                        pool.wait_ge(s["mT0"], done(n, u, 1))
                    pool.wait_ge(s["mx0_0"], done(n, u))
                    pool.wait_ge(s["mx0_1"], done(n, u))
                    nc.gpsimd.tensor_tensor(mp0[:, :, 0, :], mx0[u][:], one, ALU.mult).then_inc(s["mh0"], 1)
                    pool.wait_ge(s["mh0"], done(n, u))
                    nc.gpsimd.tensor_tensor(mr0[:], mx0[u][:], mp0[:, :, 0, :], ALU.subtract).then_inc(s["mr0"], 1)
                    pool.wait_ge(s["mr0"], done(n, u))
                    nc.gpsimd.tensor_tensor(mp0[:, :, 1, :], mr0[:], one, ALU.mult).then_inc(s["mm0"], 1)
                    pool.wait_ge(s["mm0"], done(n, u))
                    nc.gpsimd.tensor_tensor(mp0[:, :, 2, :], mr0[:], mp0[:, :, 1, :], ALU.subtract).then_inc(s["ml0"], 1)

                def p3_low(n, u):
                    cols = slice(WIDE // 2, WIDE)
                    pool.wait_ge(s["p0h_0"], done(n, u))
                    if has(n, u, 1):
                        pool.wait_ge(s["pv0"], done(n, u, 1))
                    nc.gpsimd.tensor_tensor(p0l[:, cols], p0[:, cols], p0h[:, cols], ALU.subtract).then_inc(s["p0l_pool"], 1)

                def p3_rstd(n, u):
                    if has(n, u, 2):
                        pool.wait_ge(s["rmat"], done(n, u, 2))
                        pool.wait_ge(s["g"], done(n, u, 2))
                    rstd(ve2[:], mv2[u][:, 1:2], rs2[u][:], "mv2", "ve2", "rs2", n, u)
                    if has(n, u, 1):
                        pool.wait_ge(s["x1c"], done(n, u, 1))
                    nc.gpsimd.tensor_tensor(nmean2[:], mv2[u][:, 0:1], minus1[:], ALU.mult).then_inc(s["nmean2"], 1)

                def p4_nmax(n, u):
                    pool.wait_ge(s["mx1"], done(n, u))
                    if has(n, u, 1):
                        pool.wait_ge(s["ex_1"], done(n, u, 1))
                    nc.gpsimd.tensor_tensor(nmx1[:], mx1[:], nscale[:], ALU.mult).then_inc(s["nmx1"], 1)

                def p5_rstd(n, u):
                    if has(n, u, 1):
                        pool.wait_ge(s["y"], done(n, u, 1))
                    rstd(ve3[:], mv3[:, 1:2], rs3[:], "mv3", "ve3", "rs3", n, u)

                def p5_bias(n, u):
                    pool.wait_ge(s["x2s"], done(n, u))
                    if has(n, u, 1):
                        pool.wait_ge(s["y"], done(n, u, 1))
                    nc.gpsimd.tensor_tensor(x2b[:], x2s[:], fbias[:], ALU.add).then_inc(s["x2b"], 1)

                if n[1] is not None:
                    p1_q(n[1], 1 - r)
                if n[2] is not None:
                    p2_split(n[2], r)
                if n[0] is not None:
                    p0_rstd(n[0], r)
                if n[4] is not None:
                    p4_nmax(n[4], r)
                if n[3] is not None:
                    p3_low(n[3], 1 - r)
                if n[5] is not None:
                    p5_bias(n[5], 1 - r)
                if n[5] is not None:
                    p5_rstd(n[5], 1 - r)
                if n[1] is not None:
                    p1_values(n[1], 1 - r)
                if n[3] is not None:
                    p3_rstd(n[3], 1 - r)
                if n[1] is not None:
                    p1_residual(n[1], 1 - r)

            run(pool, step, {1: masks,
                             5: lambda: pool.wait_ge(s["ld_ffn"], 16 * 8)})

        @block.scalar
        def _(act):
            act.dma_start(xin[0][:], x_d[0:P, :]).then_inc(ld_x[0], 16)
            act.dma_start(wvu[:], io["L0_attn_Wv_u"]).then_inc(s["ld_vu"], 16)
            act.dma_start(bvr[:], io["L0_attn_bv_u"].rearrange("(c p) -> c p", p=P)).then_inc(s["ld_vu"], 16)
            act.dma_start(xin[1][:], x_d[P:2 * P, :]).then_inc(ld_x[1], 16)

            def attn_weights():
                act.wait_ge(s["wqdT_ps"], 1)
                nc.scalar.copy(wqdT[:], M[0][0:QL, :]).then_inc(s["wqdT"], 1)
                act.wait_ge(s["wqc_ps"], 1)
                nc.scalar.copy(wqc[:, :, 0:P], M[0][:].rearrange("p (c n) -> p c n", c=DC)).then_inc(s["wqc"], 1)
                act.wait_ge(s["bqc_ps"], 1)
                nc.scalar.copy(bqc[:, 0:P], M[1][:, 128:128 + P]).then_inc(s["bqc"], 1)

            def value_weights():
                act.wait_ge(s["wvuT_ps"], 1)
                nc.scalar.copy(vT[:], M[3][:, 0:DC * LAT + DC]).then_inc(s["wvuT"], 1)

            def out_weights():
                act.wait_ge(s["zeros"], 1)
                act.wait_ge(s["xw_ps"], 1)
                for b in range(2):
                    q_ = slice(64 * b, 64 * b + 64)
                    nc.scalar.copy(kq[q_, q_], M[1][q_, 0:64])
                    nc.scalar.copy(wvbd[q_, q_], M[1][q_, 64:128])
                    fin = nc.scalar.copy(wsbd[q_, q_], M[1][q_, 128:192])
                fin.then_inc(s["xw"], 1)
                act.wait_ge(s["mout_ps"], 1)
                nc.scalar.copy(mout[:], M[3][:]).then_inc(s["mout"], 1)

            def lora_coef():
                act.wait_ge(s["coef_ps"], 1)
                nc.scalar.mul(coef[:], M[3][:, 0:1], float(ALPHA) / RANK).then_inc(s["coef"], 1)

            def ffn_weights(k):
                act.wait_ge(s["wT_ps"], k + 1)
                nc.scalar.copy(weff[:, k], (M[2] if k == 1 else M[3])[:]).then_inc(s["wT"], 1)

            def first_ffn_weights():
                ffn_weights(0)
                ffn_weights(1)

            def step(r, n):
                def p4_load(n, u):
                    if has(n, u, 2):
                        act.wait_ge(s["gv"], done(n, u, 2))
                        act.nop(nofuse=True)
                    act.dma_start(cin[u][:], ctx_d[bass.ds((n * 2 + u) * P, P), :]).then_inc(ld_c[u], 16)

                def p0_xT(n, u):
                    act.wait_ge(s["xT"], done(n, u))
                    if has(n, u, 1):
                        act.wait_ge(s["qc_ps"], done(n, u, 1))
                    nc.scalar.copy(xnT[:].rearrange("p c t -> p (c t)"), M[0][:]).then_inc(s["xnT"], 1)

                def p1_q(n, u):
                    act.wait_ge(s["qc"], done(n, u))
                    if has(n, u, 1):
                        act.wait_ge(s["qT"], done(n, u, 1))
                        act.wait_ge(s["cbd"], done(n, u, 1))
                    nc.scalar.copy(qcp[:, 0, :], qc[:]).then_inc(s["qh"], 1)
                    if has(n, u, 1) and not has(n, u, 2):
                        lora_coef()
                    elif has(n, u, 2) and not has(n, u, 3):
                        ffn_weights(2)

                def p1_qT(n, u):
                    act.wait_ge(s["cstT"], done(n, u))
                    if has(n, u, 2):
                        act.wait_ge(q_out[u], nth(n - 1, 1))
                    nc.scalar.copy(qpart[u][:].rearrange("p b a q -> p a b q"),
                                   M[0][:].bitcast(BF16)[:, P:P + NPART * P].rearrange("p (a b q) -> p a b q", a=NPART, b=2))\
                        .then_inc(s["qpart"], 1)

                def p1_c(n, u):
                    act.wait_ge(s["cstT"], done(n, u))
                    if has(n, u, 2):
                        act.wait_ge(s["b0_0"], done(n, u, 2))
                    nc.scalar.copy(cst[u][:], M[0][:].bitcast(BF16)[:, 0:P]).then_inc(s["cst"], 1)

                def p2_max(n, u):
                    act.wait_ge(s["mT0"], done(n, u))
                    if has(n, u, 2):
                        act.wait_ge(m_out[u], nth(n - 1, 1))
                    nc.scalar.copy(mx0T[u][:], M[1][:].bitcast(BF16)[0:2 * NPART * HP, 0:P]).then_inc(s["mx0T"], 1)
                    if has(n, u, 1) and not has(n, u, 2):
                        ffn_weights(3)

                def p3_exp(n, u, k):
                    act.wait_ge(s[f"b0_{k}"], done(n, u))
                    if has(n, u, 1):
                        act.wait_ge(s["pv0"], done(n, u, 1))
                    cols = slice(k * WIDE, (k + 1) * WIDE)
                    nc.scalar.activation(p0[:, cols], W[k][:], ACT.Exp, bias=lntop[:],
                                         scale=float(LAT) ** -0.5).then_inc(s[f"e0_{k}"], 1)

                def p3_high(n, u, k):
                    cols = slice(k * WIDE, (k + 1) * WIDE)
                    act.wait_ge(s[f"e0_{k}"], done(n, u))
                    nc.scalar.copy(p0h[:, cols], p0[:, cols]).then_inc(s[f"p0h_{k}"], 1)

                def p3_ctx(n, u):
                    act.wait_ge(s["ctxTb"], done(n, u))
                    if has(n, u, 1):
                        act.wait_ge(s["o"], done(n, u, 1))
                    nc.scalar.copy(ctxT[0:64, :], M[1][0:64, 0:P]).then_inc(s["ctx_lo"], 1)
                    nc.scalar.copy(ctxT[64:128, :], M[2][64:128, 0:P]).then_inc(s["ctx_hi"], 1)

                def p4_gv(n, u):
                    act.wait_ge(s["gv"], done(n, u))
                    act.wait_ge(s["rs2"], done(n, u))
                    if has(n, u, 1):
                        act.wait_ge(s["xa"], done(n, u, 1))
                    nc.scalar.activation(g[:], M[2][:, 0:CM], ACT.Copy, scale=rs2[u][:]).then_inc(s["g"], 1)
                    if has(n, u, 2):
                        act.wait_ge(s["pv1"], done(n, u, 2))
                    nc.scalar.copy(v65[u][:, :, 0:CD], M[2][:, CM:CM + P].rearrange("p (b c) -> p b c", b=2)).then_inc(s["v"], 1)

                def p4_exp(n, u, b):
                    act.wait_ge(s["nmx1"], done(n, u))
                    if has(n, u, 1):
                        act.wait_ge(s["pT"], done(n, u, 1))
                    for c in range(DC):
                        fin = nc.scalar.activation(ex[:, b, c * P:(c + 1) * P], W[1][:, b * 512 + c * P:b * 512 + (c + 1) * P], ACT.Exp,
                                                   bias=nmx1[:, b, c:c + 1], scale=float(CD) ** -0.5)
                    fin.then_inc(s[f"ex_{b}"], 1)

                def p3_center(n, u):
                    act.wait_ge(s["nmean2"], done(n, u))
                    if has(n, u, 2):
                        act.wait_ge(s["skip"], done(n, u, 2))
                        act.wait_ge(s["xa"], done(n, u, 2))
                    nc.scalar.activation(x1c[u][:], x1[:], ACT.Identity, bias=nmean2[:]).then_inc(s["x1c"], 1)

                def p4_weights(n, u):
                    act.wait_ge(s["pT"], done(n, u))
                    if has(n, u, 1):
                        act.wait_ge(s["pv1"], done(n, u, 1))
                    nc.scalar.copy(pt[:].rearrange("p b n -> p (b n)"), W[0][:]).then_inc(s["e1"], 1)

                def p5_x2(n, u):
                    act.wait_ge(s["x2"], done(n, u))
                    if has(n, u, 1):
                        act.wait_ge(s["st3"], done(n, u, 1))
                        act.wait_ge(s["x2b"], done(n, u, 1))
                    nc.scalar.activation(x2s[:], M[3][:], ACT.Identity, bias=mv2[u][:, 0:1]).then_inc(s["x2s"], 1)

                if n[4] is not None:
                    p4_gv(n[4], r)
                if n[3] is not None:
                    p3_exp(n[3], 1 - r, 1)
                if n[1] is not None:
                    p1_q(n[1], 1 - r)
                if n[3] is not None:
                    p4_load(n[3], 1 - r)
                if n[5] is not None:
                    p5_x2(n[5], 1 - r)
                if n[3] is not None:
                    p3_high(n[3], 1 - r, 1)
                if n[3] is not None:
                    p3_exp(n[3], 1 - r, 0)
                if n[1] is not None:
                    p1_qT(n[1], 1 - r)
                if n[3] is not None:
                    p3_high(n[3], 1 - r, 0)
                if n[1] is not None:
                    p1_c(n[1], 1 - r)
                if n[2] is not None:
                    p2_max(n[2], r)
                if n[4] is not None:
                    p4_exp(n[4], r, 0)
                if n[4] is not None:
                    p4_exp(n[4], r, 1)
                if n[3] is not None:
                    p3_ctx(n[3], 1 - r)
                if n[4] is not None:
                    p4_weights(n[4], r)
                if n[0] is not None:
                    p0_xT(n[0], r)
                if n[3] is not None:
                    p3_center(n[3], 1 - r)

            run(act, step, {0: attn_weights, 1: value_weights, 2: out_weights, 3: first_ffn_weights})

        @block.vector
        def _(dve):
            for tile in (half36, half5, kq, wvbd, wsbd):
                nc.vector.memset(tile[:], 0.0)
            for u in range(2):
                nc.vector.memset(ctile[u][:], 0.0)
                nc.vector.memset(qst[u][:], 0.0)
                nc.vector.memset(v65[u][:], 1.0)
                ins = nc.vector.memset(cbd[u][:], 0.0)
            ins.then_inc(s["zeros"], 1)

            def halves_and_values():
                dve.wait_ge(s["zeros"], 1)
                for b in range(2):
                    for u in range(2):
                        nc.vector.memset(cbd[u][64 * b:64 * b + 64, 0, b, LAT:LAT + 1], 1.0)
                    nc.vector.memset(half36[64 * b:64 * b + 64, b, :], 1.0)
                    nc.vector.memset(half5[64 * b:64 * b + 64, :, b, :], 1.0)
                    for u in range(2):
                        ins = nc.vector.memset(ctile[u][64 * b:64 * b + 64, b, KROWS:KALL], -1.0)
                ins.then_inc(s["halves"], 1)
                dve.wait_ge(s["wvuT"], 1)
                dve.wait_ge(s["masks2"], 1)
                for c in range(DC):
                    ins = nc.vector.tensor_tensor(vbd[:, c], hmask[:, c].unsqueeze(2).broadcast_to([P, H, LAT]),
                                                  wvuT[:, c].unsqueeze(1).broadcast_to([P, H, LAT]), ALU.mult)
                ins.then_inc(s["vbd"], 1)

            def out_weights():
                dve.wait_ge(s["cvec_ps"], 1)
                nc.vector.tensor_tensor(cvec[:], M[2][:], bo[:], ALU.add).then_inc(s["cvec"], 1)

            def ffn_weights():
                dve.wait_ge(s["coef"], 1)
                dve.wait_ge(s["lbT_ps"], 1)
                nc.vector.tensor_scalar(lbT[:], M[2][:], coef[:], None, ALU.mult).then_inc(s["lbT"], 1)

            def ffn_center(chunks):
                dve.wait_ge(s["wmean_ps"], 1)
                for k in chunks:
                    nc.vector.tensor_tensor(weff[:, k], weff[:, k], M[3][:], ALU.subtract).then_inc(s["wcen"], 1)

            def step(r, n):
                def p0_norm(n, u):
                    dve.wait_ge(ld_x[u], nth(n, 1))
                    nc.vector.bn_stats(st1[:], xin[u][:]).then_inc(s["st1"], 1)
                    dve.wait_ge(s["st1"], done(n, u))
                    dve.nop(nofuse=True)
                    nc.vector.bn_aggr(mv1[:], st1[:]).then_inc(s["mv1"], 1)

                def p0_xn(n, u):
                    dve.wait_ge(s["rs1"], done(n, u))
                    if has(n, u, 2):
                        dve.wait_ge(s["xT"], done(n, u, 2))
                    nc.vector.tensor_scalar(xn[u][:], xin[u][:], mv1[:, 0:1], rs1[:, 0:1], ALU.subtract, ALU.mult).then_inc(s["xn"], 1)

                def p1_qc(n, u):
                    dve.wait_ge(s["qc_ps"], done(n, u))
                    if not has(n, u, 1):
                        dve.wait_ge(s["bqc"], 1)
                    if has(n, u, 1):
                        dve.wait_ge(s["qr"], done(n, u, 1))
                        dve.wait_ge(s["qh"], done(n, u, 1))
                    nc.vector.tensor_tensor(qc[:], M[0][:, 0:P + LAT], bqc[:], ALU.add).then_inc(s["qc"], 1)

                def p2_max(n, u, b):
                    dve.wait_ge(s[f"a0_{b}"], done(n, u))
                    if has(n, u, 2):
                        dve.wait_ge(s["ml0"], done(n, u, 2))
                    nc.vector.tensor_reduce(mx0[u][:, b, :], W[b][:].rearrange("p (h k) -> p h k", k=S), AX_X, ALU.max)\
                        .then_inc(s[f"mx0_{b}"], 1)
                    if b == 0 and not has(n, u, 1):
                        ffn_weights()

                def p3_ctx(n, u):
                    if has(n, u, 1) and not has(n, u, 2):
                        ffn_center((0, 1))
                    dve.wait_ge(s["pv0"], done(n, u))
                    nc.vector.tensor_reduce(pv5[:].rearrange("p h b j -> p h (b j)"),
                                            M[1][:, 0:HP * NPART * 2 * (LAT + 1)].rearrange("p (h k m) -> p h m k", h=HP, k=NPART),
                                            AX_X, ALU.add).then_inc(s["pv5"], 1)
                    pv = pv5[:].rearrange("p h b j -> p b h j")
                    dve.wait_ge(s["pv5"], done(n, u))
                    nc.vector.reciprocal(rden0[:], pv[:, :, :, LAT]).then_inc(s["rden0"], 1)
                    dve.wait_ge(s["rden0"], done(n, u))
                    if has(n, u, 1):
                        dve.wait_ge(s["ctxTb"], done(n, u, 1))
                    nc.vector.tensor_tensor(ctxn[:], pv[:, :, :, 0:LAT],
                                            rden0[:].unsqueeze(3).broadcast_to([P, 2, HP, LAT]), ALU.mult).then_inc(s["ctxn"], 1)

                def p3_low(n, u, k):
                    cols = slice(k * WIDE, (k + 1) * WIDE if k else WIDE // 2)
                    dve.wait_ge(s[f"p0h_{k}"], done(n, u))
                    nc.vector.tensor_tensor(p0l[:, cols], p0[:, cols], p0h[:, cols], ALU.subtract).then_inc(s[f"p0l_{k}"], 1)

                def p3_x1(n, u):
                    dve.wait_ge(s["o"], done(n, u))
                    dve.wait_ge(s["x0b"], done(n, u))
                    if has(n, u, 1):
                        dve.wait_ge(s["x1c"], done(n, u, 1))
                    nc.vector.tensor_tensor(x1[:], M[2][:], x0b[u][:], ALU.add).then_inc(s["x1"], 1)
                    dve.wait_ge(s["x1"], done(n, u))
                    nc.vector.bn_stats(st2[:], x1[:]).then_inc(s["st2"], 1)
                    dve.wait_ge(s["st2"], done(n, u))
                    if has(n, u, 2):
                        dve.wait_ge(s["x2s"], done(n, u, 2))
                    dve.nop(nofuse=True)
                    nc.vector.bn_aggr(mv2[u][:], st2[:]).then_inc(s["mv2"], 1)

                def p4_max(n, u):
                    dve.wait_ge(s["xa"], done(n, u))
                    if has(n, u, 1):
                        dve.wait_ge(s["nmx1"], done(n, u, 1))
                    nc.vector.tensor_reduce(mx1[:].rearrange("p b c -> p (b c)"), W[1][:].rearrange("p (c m) -> p c m", m=CM),
                                            AX_X, ALU.max).then_inc(s["mx1"], 1)

                def p4_rmat(n, u):
                    if not has(n, u, 1):
                        ffn_center((2, 3))
                    dve.wait_ge(s["rs2"], done(n, u))
                    if has(n, u, 1):
                        dve.wait_ge(s["skip"], done(n, u, 1))
                    nc.vector.scalar_tensor_tensor(rmat[:], wsbd[:], rs2[u][:], identf[:], ALU.mult, ALU.add).then_inc(s["rmat"], 1)

                def p4_x2(n, u):
                    pv = W[0][:].rearrange("p (b m) -> p b m", b=2)[:, :, 0:DC * (CD + 1)].rearrange("p b (c k) -> p b c k", c=DC)
                    dve.wait_ge(s["pv1"], done(n, u))
                    nc.vector.reciprocal(rden1[:], pv[:, :, :, CD]).then_inc(s["rden1"], 1)
                    dve.wait_ge(s["rden1"], done(n, u))
                    for b in range(2):
                        ins = nc.vector.tensor_tensor(pvn[:, :, b, :], pv[:, b, :, 0:CD],
                                                      rden1[:, b, :].unsqueeze(2).broadcast_to([P, DC, CD]), ALU.mult)
                    ins.then_inc(s["pvn"], 1)
                    dve.wait_ge(s["pvn"], done(n, u))
                    dve.wait_ge(s["skip"], done(n, u))
                    if has(n, u, 2):
                        dve.wait_ge(s["ffn"], done(n, u, 2))
                    nc.vector.tensor_tensor(x2T[u][:].rearrange("p c t -> p (c t)"), M[1][:],
                                            pvn[:].rearrange("p c b k -> p (c b k)"), ALU.add).then_inc(s["x2T"], 1)

                def p5_stats(n, u):
                    dve.wait_ge(s["x2s"], done(n, u))
                    nc.vector.bn_stats(st3[:], x2s[:]).then_inc(s["st3"], 1)
                    dve.wait_ge(s["st3"], done(n, u))
                    if has(n, u, 1):
                        dve.wait_ge(s["ve3"], done(n, u, 1))
                    dve.nop(nofuse=True)
                    nc.vector.bn_aggr(mv3[:], st3[:]).then_inc(s["mv3"], 1)

                def p5_y(n, u):
                    dve.wait_ge(s["ffn"], done(n, u))
                    dve.wait_ge(s["rs3"], done(n, u))
                    dve.wait_ge(s["x2b"], done(n, u))
                    if has(n, u, 2):
                        dve.wait_ge(y_out[u], nth(n - 1, 1))
                    nc.vector.scalar_tensor_tensor(y[u][:], M[3][:, 0:D], rs3[:], x2b[:], ALU.mult, ALU.add).then_inc(s["y"], 1)

                def p5_y_halves(n, u):
                    dve.wait_ge(s["rs3"], done(n, u))
                    dve.wait_ge(s["x2b"], done(n, u))
                    dve.wait_ge(y_out[u], nth(n - 1, 1))
                    for k in range(2):
                        cols, at = half_of(k)
                        dve.wait_ge(s["ffn_half"], k + 1)
                        dve.nop(nofuse=True)
                        nc.vector.scalar_tensor_tensor(y[u][:, cols], W[1][:, at], rs3[:], x2b[:, cols],
                                                       ALU.mult, ALU.add).then_inc(s["y_half"], 1)

                if n[1] is not None:
                    p1_qc(n[1], 1 - r)
                if n[2] is not None:
                    p2_max(n[2], r, 0)
                if n[0] is not None:
                    p0_norm(n[0], r)
                if n[4] is not None:
                    p4_max(n[4], r)
                if n[3] is not None:
                    p3_low(n[3], 1 - r, 1)
                if n[3] is not None:
                    p3_low(n[3], 1 - r, 0)
                if n[5] is not None:
                    p5_stats(n[5], 1 - r)
                if n[3] is not None:
                    p3_ctx(n[3], 1 - r)
                if n[0] is not None:
                    p0_xn(n[0], r)
                if n[5] is not None and last(n[5], 1 - r):
                    p5_y_halves(n[5], 1 - r)
                elif n[5] is not None:
                    p5_y(n[5], 1 - r)
                if n[4] is not None:
                    p4_rmat(n[4], r)
                if n[3] is not None:
                    p3_x1(n[3], 1 - r)
                if n[1] is not None:
                    p2_max(n[1], 1 - r, 1)
                if n[4] is not None:
                    p4_x2(n[4], r)

            run(dve, step, {1: halves_and_values, 2: out_weights})

        @block.tensor
        def _(pe):
            mm = nc.tensor.matmul
            tr = nc.tensor.transpose

            def attn_weights():
                pe.wait_ge(s["identf"], 1)
                pe.wait_ge(s["ld_wqd"], 16)
                for c in range(DC):
                    ins = tr(M[0][0:QL, c * P:(c + 1) * P], wqd[:, c], identf[:])
                ins.then_inc(s["wqdT_ps"], 1)
                pe.wait_ge(s["w13p"], 1)
                pe.wait_ge(s["wqdT"], 1)
                for c in range(DC):
                    ins = mm(M[0][:, c * P:(c + 1) * P], wqdT[:, c * P:(c + 1) * P], w13p[0:QL, :], start=True, stop=True)
                ins.then_inc(s["wqc_ps"], 1)
                pe.wait_ge(s["ld_attn"], 48)
                mm(M[1][:, 128:128 + P], bq13[:].broadcast_to([QL + 1, P]), w13p[:], start=True, stop=True).then_inc(s["bqc_ps"], 1)
                pe.wait_ge(s["wqc"], 1)

            def value_weights():
                pe.wait_ge(s["ident"], 1)
                pe.wait_ge(s["ld_vu"], 32)
                for c in range(DC):
                    ins = tr(M[3][:, c * LAT:(c + 1) * LAT], wvu[:, c * P:(c + 1) * P], identf[0:LAT, 0:LAT])
                ins = tr(M[3][:, DC * LAT:DC * LAT + DC], bvr[:], identf[0:DC, 0:DC])
                ins.then_inc(s["wvuT_ps"], 1)

            def out_weights():
                pe.wait_ge(s["bqc"], 1)
                pe.wait_ge(s["ld_x"], 112)
                mm(M[1][:, 0:CD], xwk[:].rearrange("p a b -> p (a b)"), xwq[:], start=True, stop=True)
                tr(M[1][:, 64:128], xwv[:].rearrange("p a b -> p (a b)"), identf[0:CD, 0:CD])
                tr(M[1][:, 128:192], xws[:].rearrange("p a b -> p (a b)"), identf[0:CD, 0:CD]).then_inc(s["xw_ps"], 1)
                pe.wait_ge(s["ld_vo"], 32)
                pe.wait_ge(s["vbd"], 1)
                for c in range(DC):
                    ins = mm(M[3][:], vbd[:, c].rearrange("p h j -> p (h j)"), wo[:, c], start=(c == 0), stop=(c == DC - 1))
                ins.then_inc(s["mout_ps"], 1)
                for c in range(DC):
                    ins = mm(M[2][:], bvT[:, c:c + 1].broadcast_to([P, P]), wo[:, c], start=(c == 0), stop=(c == DC - 1))
                ins.then_inc(s["cvec_ps"], 1)

            def lora_b():
                pe.wait_ge(s["ld_ffn"], 128)
                pe.wait_ge(s["masks2"], 1)
                pe.wait_ge(s["mout"], 1)
                mm(M[3][:, 0:1], spread[:], lw[:], start=True, stop=True).then_inc(s["coef_ps"], 1)
                pe.wait_ge(s["cvec"], 1)
                for c in range(DC):
                    ins = tr(M[2][:, c * P:(c + 1) * P], lb[:, c].rearrange("p n r -> p (n r)"), identf[:])
                ins.then_inc(s["lbT_ps"], 1)

            def ffn_weights(k):
                pe.wait_ge(s["lbT"], 1)
                if k >= 2:
                    pe.wait_ge(s["wT"], 1 if k == 2 else 3)
                bank = M[2] if k == 1 else M[3]
                mm(bank[:], la[:, k * P:(k + 1) * P], lbT[:], start=True, stop=False)
                for c in range(DC):
                    ins = mm(bank[:, c * P:(c + 1) * P], fw[:, c, k * P:(k + 1) * P], identf[:], start=False, stop=(c == DC - 1))
                ins.then_inc(s["wT_ps"], 1)

            def ffn_mean():
                pe.wait_ge(s["wT"], DC)
                for k in range(DC):
                    ins = mm(M[3][:], meanw[:], weff[:, k], start=(k == 0), stop=(k == DC - 1))
                ins.then_inc(s["wmean_ps"], 1)

            def ffn_centered():
                pe.wait_ge(s["wcen"], DC)

            def step(r, n):
                def p0_xT(n, u):
                    pe.wait_ge(s["xn"], done(n, u))
                    if has(n, u, 1):
                        pe.wait_ge(s["cst"], done(n, u, 1))
                    for c in range(DC):
                        ins = tr(M[0][:, c * P:(c + 1) * P], xn[u][:, c * P:(c + 1) * P], identf[:])
                    ins.then_inc(s["xT"], 1)

                def p1_qc(n, u):
                    pe.wait_ge(s["xnT"], done(n, u))
                    for c in range(DC):
                        ins = mm(M[0][:, 0:P + LAT], xnT[:, c], wqc[:, c], start=(c == 0), stop=(c == DC - 1))
                    ins.then_inc(s["qc_ps"], 1)

                def p1_cT(n, u):
                    pe.wait_ge(s["ql"], done(n, u))
                    for k in range(NPART):
                        ins = tr(M[0][:].bitcast(BF16)[:, (1 + k) * P:(2 + k) * P], qcp[:, k, 0:P], ident[:])
                    ins.then_inc(s["qT"], 1)
                    pe.wait_ge(s["ctile"], done(n, u))
                    tr(M[0][:].bitcast(BF16)[:, 0:P], ctile[u][:].rearrange("p b k -> p (b k)"), ident[:]).then_inc(s["cstT"], 1)

                def p2_scores(n, u, b):
                    if b == 1 and not has(n, u, 1):
                        out_weights()
                    elif b == 1 and not has(n, u, 2):
                        ffn_weights(0)
                        ffn_weights(1)
                    if has(n, u, 3):
                        pe.wait_ge(s["pvn" if b == 0 else "ex_1"], done(n, u, 3))
                    elif has(n, u, 2):
                        pe.wait_ge(s[f"e0_{b}"], done(n, u, 2))
                    elif has(n, u, 1):
                        pe.wait_ge(s[f"mx0_{b}"], done(n, u, 1))
                    pe.wait_ge(q_in[u][b], nth(n, 3))
                    pe.wait_ge(s["cst"], done(n, u))
                    rows = slice(64 * b, 64 * b + KROWS)
                    for h in range(HP):
                        ins = mm(W[b][:, h * S:(h + 1) * S], qst[u][rows, h * P:(h + 1) * P], cst[u][rows, 64 * b:64 * b + 64],
                                 start=True, stop=True)
                    ins.then_inc(s[f"a0_{b}"], 1)
                    if b == 0 and not has(n, u, 1):
                        lora_b()
                    elif b == 0 and not has(n, u, 2):
                        ffn_weights(2)

                def p2_maxT(n, u):
                    if has(n, u, 3):
                        pe.wait_ge(s["x2T"], done(n, u, 3))
                    elif has(n, u, 2):
                        pe.wait_ge(s["ctx_lo"], done(n, u, 2))
                    elif has(n, u, 1):
                        pe.wait_ge(s["mx0T"], done(n, u, 1))
                    else:
                        pe.wait_ge(s["xw"], 1)
                    pe.wait_ge(s["ml0"], done(n, u))
                    tr(M[1][:].bitcast(BF16)[0:2 * NPART * HP, 0:P], mp0[:].rearrange("p b a h -> p (b a h)"), ident[:])\
                        .then_inc(s["mT0"], 1)

                def p3_scores(n, u, k):
                    if not last(n, u):
                        pe.wait_ge(s[f"mx0_{k}"], done(n, u, -1))
                    else:
                        pe.wait_ge(s["pvn" if k == 0 else "ex_1"], done(n, u, 2))
                    pe.wait_ge(m_in[u], nth(n, 2))
                    for c in range(2):
                        col = k * WIDE + c * 512
                        ins = mm(W[k][:, c * 512:(c + 1) * 512], cst[u][0:64 + KALL, :], qst[u][0:64 + KALL, col:col + 512],
                                 start=True, stop=True)
                    ins.then_inc(s[f"b0_{k}"], 1)

                def p3_values(n, u, k):
                    if k == 1:
                        if not has(n, u, 1):
                            ffn_weights(3)
                        elif not has(n, u, 2):
                            ffn_mean()
                        if not last(n, u):
                            pe.wait_ge(s["mx0T"], done(n, u, -1))
                        else:
                            pe.wait_ge(s["x2T"], done(n, u, 2))
                        pe.wait_ge(s["cbd"], done(n, u))
                    pe.wait_ge(s[f"p0l_{k}"], done(n, u))
                    width = NPART * 2 * (LAT + 1)
                    for h in range(k * HP // 2, (k + 1) * HP // 2):
                        if h == HP // 4:
                            pe.wait_ge(s["p0l_pool"], done(n, u))
                        for part in (p0h, p0l):
                            ins = mm(M[1][:, h * width:(h + 1) * width], part[:, h * P:(h + 1) * P],
                                     cbd[u][:].rearrange("p k b j -> p (k b j)"), start=(part is p0h), stop=(part is p0l))
                    if k == 0:
                        ins.then_inc(s["pv0"], 1)

                def p3_ctxT(n, u):
                    pe.wait_ge(s["ctxn"], done(n, u))
                    if has(n, u, 1):
                        pe.wait_ge(s["v"], done(n, u, 1))
                    else:
                        pe.wait_ge(s["wT"], 2)
                    pe.nop(nofuse=True)
                    for k in range(2):
                        rows = slice(64 * k, 64 * k + 64)
                        for b in range(2):
                            ins = mm(M[1 + k][rows, b * 64:b * 64 + 64], ctxn[rows, b].rearrange("p h j -> p (h j)"),
                                     identf[rows, 64 * k:64 * k + 64], start=True, stop=True)
                        ins.then_inc(s["ctxTa" if k == 0 else "ctxTb"], 1)

                def p3_out(n, u):
                    pe.wait_ge(s["ctx_lo"], done(n, u))
                    pe.wait_ge(s["ctx_hi"], done(n, u))
                    if not has(n, u, 1):
                        pe.wait_ge(s["mout"], 1)
                    mm(M[2][:], ctxT[:], mout[:], start=True, stop=True).then_inc(s["o"], 1)

                def p4_gv(n, u):
                    pe.wait_ge(s["x1"], done(n, u))
                    pe.wait_ge(ld_c[u], nth(n, 1))
                    mm(M[2][:, 0:CM], kq[:], cin[u][:], start=True, stop=True)
                    mm(M[2][:, CM:CM + P], cin[u][:], wvbd[:], start=True, stop=True).then_inc(s["gv"], 1)

                def p4_energy(n, u):
                    if not last(n, u):
                        pe.wait_ge(s["e0_1"], done(n, u, -1))
                    else:
                        pe.wait_ge(s["ex_1"], done(n, u, 1))
                    pe.wait_ge(s["g"], done(n, u))
                    pe.wait_ge(s["x1c"], done(n, u))
                    for b in range(2):
                        rows = slice(64 * b, 64 * b + 64)
                        for c in range(DC):
                            col = b * 512 + c * P
                            ins = mm(W[1][:, col:col + P], x1c[u][rows, c * P:(c + 1) * P], g[rows, :], start=True, stop=True)
                    ins.then_inc(s["xa"], 1)

                def p4_turn(n, u, b):
                    if not last(n, u):
                        pe.wait_ge(s["e0_0"], done(n, u, -1))
                    else:
                        pe.wait_ge(s["pvn"], done(n, u, 1))
                    pe.wait_ge(s[f"ex_{b}"], done(n, u))
                    for c in range(DC):
                        ins = tr(W[0][:, b * 512 + c * P:b * 512 + (c + 1) * P], ex[:, b, c * P:(c + 1) * P], identf[:])
                    if b == 1:
                        ins.then_inc(s["pT"], 1)

                def p4_skip(n, u):
                    if not last(n, u):
                        pe.wait_ge(s["ctx_lo"], done(n, u, -1))
                    else:
                        pe.wait_ge(s["x2T"], done(n, u, 1))
                    pe.wait_ge(s["rmat"], done(n, u))
                    for c in range(DC):
                        ins = mm(M[1][:, c * P:(c + 1) * P], x1c[u][:, c * P:(c + 1) * P], rmat[:], start=True, stop=True)
                    ins.then_inc(s["skip"], 1)

                def p4_values(n, u):
                    pe.wait_ge(s["e1"], done(n, u))
                    pe.wait_ge(s["v"], done(n, u))
                    for b in range(2):
                        for c in range(DC):
                            col = b * 512 + c * (CD + 1)
                            ins = mm(W[0][:, col:col + CD + 1], pt[:, b, c * P:(c + 1) * P], v65[u][:, b, :], start=True, stop=True)
                    ins.then_inc(s["pv1"], 1)

                def p5_x2(n, u):
                    pe.wait_ge(s["x2T"], done(n, u))
                    if has(n, u, 1):
                        pe.wait_ge(s["y"], done(n, u, 1))
                    for c in range(DC):
                        ins = tr(M[3][:, c * P:(c + 1) * P], x2T[u][:, c, :], identf[:])
                    ins.then_inc(s["x2"], 1)

                def p5_ffn(n, u, c):
                    if c == 0:
                        pe.wait_ge(s["x2s"], done(n, u))
                    ins = mm(M[3][:, 0:D], x2T[u][:, c, :], weff[:, c], start=(c == 0), stop=(c == DC - 1))
                    if c == DC - 1:
                        ins.then_inc(s["ffn"], 1)

                def p5_ffn_halves(n, u):
                    for k in range(2):
                        cols, at = half_of(k)
                        for c in range(DC):
                            ins = mm(W[1][:, at], x2T[u][:, c, :], weff[:, c, cols], start=(c == 0), stop=(c == DC - 1))
                        ins.then_inc(s["ffn_half"], 1)

                if n[4] is not None:
                    p4_gv(n[4], r)
                if n[3] is not None:
                    p3_scores(n[3], 1 - r, 1)
                if n[1] is not None:
                    p1_qc(n[1], 1 - r)
                if n[2] is not None:
                    p2_scores(n[2], r, 0)
                elif n[3] is not None:
                    p3_scores(n[3], 1 - r, 0)
                    p5_x2(n[5], 1 - r)
                if n[5] is not None and n[2] is not None:
                    p5_x2(n[5], 1 - r)
                if n[4] is not None:
                    p4_energy(n[4], r)
                if n[5] is not None and n[3] is None:
                    p5_x2(n[5], 1 - r)
                if n[3] is not None and n[2] is not None:
                    p3_scores(n[3], 1 - r, 0)
                if n[1] is not None:
                    p1_cT(n[1], 1 - r)
                ends = n[5] is not None and last(n[5], 1 - r)
                if ends:
                    p5_ffn_halves(n[5], 1 - r)
                elif n[5] is not None:
                    p5_ffn(n[5], 1 - r, 0)
                    p5_ffn(n[5], 1 - r, 1)
                if n[2] is not None:
                    p2_maxT(n[2], r)
                if n[5] is not None and not ends:
                    p5_ffn(n[5], 1 - r, 2)
                if n[3] is not None:
                    p3_values(n[3], 1 - r, 1)
                if n[3] is not None:
                    p3_values(n[3], 1 - r, 0)
                if n[5] is not None and not ends:
                    p5_ffn(n[5], 1 - r, 3)
                if n[4] is not None:
                    p4_turn(n[4], r, 0)
                if n[3] is not None:
                    p3_ctxT(n[3], 1 - r)
                if n[0] is not None:
                    p0_xT(n[0], r)
                if n[4] is not None:
                    p4_turn(n[4], r, 1)
                if n[3] is not None:
                    p3_out(n[3], 1 - r)
                if n[1] is not None:
                    p2_scores(n[1], 1 - r, 1)
                if n[4] is not None:
                    p4_skip(n[4], r)
                if n[4] is not None:
                    p4_values(n[4], r)

            run(pe, step, {0: attn_weights, 1: value_weights, 5: ffn_centered})


_INS = ["x", "ctx_1024", "L0_attn_Wq_d", "L0_attn_bq_d", "L0_attn_W_qk", "L0_attn_b_qk", "L0_attn_Wkv_d",
        "L0_attn_bkv_d", "L0_attn_Wv_u", "L0_attn_bv_u", "L0_attn_Wo", "L0_attn_bo", "L0_xattn_Wq", "L0_xattn_Wk",
        "L0_xattn_Wv", "L0_xattn_Wskip", "L0_ffn_lora_A", "L0_ffn_lora_B", "L0_ffn_W", "L0_ffn_bias",
        "L0_ffn_lora_weights"]


def kernel(**inputs):
    import numpy as _np
    import concourse.bacc as _bacc
    from concourse import mybir as _mybir
    from concourse.bass_utils import run_bass_kernel_spmd as _run

    nc = _bacc.Bacc("TRN2", target_bir_lowering=False, num_devices=1)
    arrays, io = {}, {}
    for name in _INS:
        a = _np.ascontiguousarray(inputs[name])
        arrays[f"in_{name}"] = a
        io[name] = nc.dram_tensor(f"in_{name}", a.shape, _mybir.dt.from_np(a.dtype), kind="ExternalInput").ap()
    io["out"] = nc.dram_tensor("out_y", inputs["x"].shape, _mybir.dt.float32, kind="ExternalOutput").ap()
    decoder(nc, io)
    r = _run(nc, [arrays], core_ids=[0])
    return r.results[0]["out_y"]
```
